# Optimizing a Trainium2 kernel written in Bass

```python
import numpy as np
import jax
import jax.numpy as jnp

def _softmax(x, axis=-1):
    return jax.nn.softmax(x, axis=axis)

def _gelu(x):
    return jax.nn.gelu(x, approximate=True)

def _silu(x):
    return jax.nn.silu(x)

def _sigmoid(x):
    return jax.nn.sigmoid(x)

def _layernorm(x, axis=-1, eps=1e-05):
    m = jnp.mean(x, axis=axis, keepdims=True)
    v = jnp.var(x, axis=axis, keepdims=True)
    return (x - m) / jnp.sqrt(v + eps)

def _scatter_add(tgt, idx, src, axis=0):
    return tgt.at[idx].add(src)

def _segment_sum(src, seg, n):
    return jax.ops.segment_sum(src, seg, n)
kernel_name = 'mk_flamingo_gated_d1_seqx_r4_252bfd'

def setup_inputs(seed: int=0):
    np.random.seed(seed)
    _w = jnp.asarray

    def _rec_inputs():
        import jax
        import jax.numpy as jnp
        _rk = jax.random.key(seed)
        x = -0.000125 + 0.9999 * jax.random.normal(jax.random.fold_in(_rk, 1), (16, 128, 256), jnp.float32)
        _lenS = 128 - jax.random.randint(jax.random.fold_in(_rk, 7), (16,), 0, max(1, 128 // 4) + 1, jnp.int32)
        _lenS2 = 128 - jax.random.randint(jax.random.fold_in(_rk, 8), (16,), 0, max(1, 128 // 4) + 1, jnp.int32)
        _ctx_2048P = jax.random.normal(jax.random.fold_in(_rk, 11), (16, 16, 512), jnp.float32)
        _ctx_2048c = jax.random.dirichlet(jax.random.fold_in(_rk, 511), 0.3 * jnp.ones((16,), jnp.float32), (16, 128))
        _ctx_2048t = jnp.einsum('bsk,bkd->bsd', _ctx_2048c, _ctx_2048P)
        _ctx_2048t = _ctx_2048t * jax.lax.rsqrt(jnp.mean(jnp.square(_ctx_2048t)) + 1e-12) * 0.953939
        ctx_2048 = -1.39393e-06 + 0.999914 * (_ctx_2048t + 0.3 * jax.random.normal(jax.random.fold_in(_rk, 611), (16, 128, 512), jnp.float32))
        _g = jax.random.normal(jax.random.fold_in(_rk, 9001), (2, 1), jnp.float32)
        _g = jnp.sign(_g) * jnp.maximum(jnp.abs(_g), 1.0) + (_g == 0) * 1.0
        g_xattn = _g[0]
        g_ffn = _g[1]
        return (x, ctx_2048, g_xattn, g_ffn)
    x, ctx_2048, g_xattn, g_ffn = _rec_inputs()

    def _L0_xattn_setup():
        import jax, jax.numpy as jnp
        import numpy as np
        B, N, DIM = (8, 1024, 256)
        M, CTX = (64, 512)
        HEADS, DH = (16, 64)
        INNER = HEADS * DH
        EPS = 1e-06

        def _split_heads(t):
            b, n, _ = t.shape
            return t.reshape(b, n, HEADS, DH).transpose(0, 2, 1, 3)
        key = jax.random.key(seed)
        ks = jax.random.split(key, 6)
        x = jax.random.normal(ks[0], (B, N, DIM), dtype=jnp.float32)
        context = jax.random.normal(ks[1], (B, M, CTX), dtype=jnp.float32)
        Wq = jax.random.normal(ks[2], (DIM, INNER), dtype=jnp.float32) / np.sqrt(DIM)
        Wkv = jax.random.normal(ks[3], (CTX, 2 * INNER), dtype=jnp.float32) / np.sqrt(CTX)
        null_kv = jax.random.normal(ks[4], (2, DH), dtype=jnp.float32) / np.sqrt(2.0)
        Wout = jax.random.normal(ks[5], (INNER, DIM), dtype=jnp.float32) / np.sqrt(INNER)
        ln_scale = jnp.ones((DIM,), dtype=jnp.float32)
        ln_bias = jnp.zeros((DIM,), dtype=jnp.float32)
        return {'x': x, 'context': context, 'Wq': Wq, 'Wkv': Wkv, 'null_kv': null_kv, 'Wout': Wout, 'ln_scale': ln_scale, 'ln_bias': ln_bias}
    _L0_xattn_all = _L0_xattn_setup()
    _L0_xattn_in = {k: v for k, v in _L0_xattn_all.items() if k in ('Wq', 'Wkv', 'null_kv', 'Wout', 'ln_scale', 'ln_bias')}
    del _L0_xattn_all

    def _L0_ffn_setup():
        import jax, jax.numpy as jnp
        import numpy as np
        BLOCK = 32
        W_BITS = 4
        ACT_BITS = 16

        def act_qdq(x):
            qmax = 2.0 ** (ACT_BITS - 1) - 1.0
            scale = jnp.maximum(jnp.max(jnp.abs(x)) / qmax, 1e-12)
            return jnp.clip(jnp.round(x / scale), -qmax - 1.0, qmax) * scale

        def fixed_qdq_u16(x):
            scale = 1.0 / 65536.0
            return jnp.clip(jnp.round(x / scale), 0.0, 65535.0) * scale

        def lpbq_dequant(w):
            O, I = w.shape
            qmax = 2.0 ** (W_BITS - 1) - 1.0
            wb = w.reshape(O, I // BLOCK, BLOCK)
            s = jnp.maximum(jnp.max(jnp.abs(wb), axis=-1, keepdims=True) / qmax, 1e-12)
            wq = jnp.clip(jnp.round(wb / s), -qmax - 1.0, qmax) * s
            return wq.reshape(O, I)
        key = jax.random.key(seed)
        k1, k2, k3, k4 = jax.random.split(key, 4)
        B, S, H, I = (2, 1024, 256, 768)
        x = jax.random.normal(k1, (B, S, H), jnp.float32)
        w_gate = jax.random.normal(k2, (I, H), jnp.float32) * 0.02
        w_up = jax.random.normal(k3, (I, H), jnp.float32) * 0.02
        w_down = jax.random.normal(k4, (H, I), jnp.float32) * 0.02
        return {'x': x, 'w_gate': w_gate, 'w_up': w_up, 'w_down': w_down}
    _L0_ffn_all = _L0_ffn_setup()
    _L0_ffn_in = {k: v for k, v in _L0_ffn_all.items() if k in ('w_gate', 'w_up', 'w_down')}
    del _L0_ffn_all
    return {'x': x, 'ctx_2048': ctx_2048, 'g_xattn': g_xattn, 'g_ffn': g_ffn, 'L0_xattn_Wq': _L0_xattn_in['Wq'], 'L0_xattn_Wkv': _L0_xattn_in['Wkv'], 'L0_xattn_null_kv': _L0_xattn_in['null_kv'], 'L0_xattn_Wout': _L0_xattn_in['Wout'], 'L0_xattn_ln_scale': _L0_xattn_in['ln_scale'], 'L0_xattn_ln_bias': _L0_xattn_in['ln_bias'], 'L0_ffn_w_gate': _L0_ffn_in['w_gate'], 'L0_ffn_w_up': _L0_ffn_in['w_up'], 'L0_ffn_w_down': _L0_ffn_in['w_down']}

def reference(x, ctx_2048, g_xattn, g_ffn, L0_xattn_Wq, L0_xattn_Wkv, L0_xattn_null_kv, L0_xattn_Wout, L0_xattn_ln_scale, L0_xattn_ln_bias, L0_ffn_w_gate, L0_ffn_w_up, L0_ffn_w_down):
    import jax
    import jax.numpy as jnp

    def _L0_xattn_ref(x, context, Wq, Wkv, null_kv, Wout, ln_scale, ln_bias):
        import jax, jax.numpy as jnp
        import numpy as np
        B, N, DIM = (8, 1024, 256)
        M, CTX = (64, 512)
        HEADS, DH = (16, 64)
        INNER = HEADS * DH
        EPS = 1e-06

        def _split_heads(t):
            b, n, _ = t.shape
            return t.reshape(b, n, HEADS, DH).transpose(0, 2, 1, 3)
        scale = DH ** (-0.5)
        b = x.shape[0]
        q = _split_heads(jnp.einsum('bnd,df->bnf', x, Wq))
        kv = jnp.einsum('bmc,cf->bmf', context, Wkv)
        k, v = jnp.split(kv, 2, axis=-1)
        k, v = (_split_heads(k), _split_heads(v))
        nk = jnp.broadcast_to(null_kv[0], (b, HEADS, 1, DH))
        nv = jnp.broadcast_to(null_kv[1], (b, HEADS, 1, DH))
        k = jnp.concatenate((nk, k), axis=-2)
        v = jnp.concatenate((nv, v), axis=-2)
        q = q * scale
        sim = jnp.einsum('bhid,bhjd->bhij', q, k)
        attn = jax.nn.softmax(sim, axis=-1)
        out = jnp.einsum('bhij,bhjd->bhid', attn, v)
        out = out.transpose(0, 2, 1, 3).reshape(b, -1, INNER)
        out = jnp.einsum('bnf,fd->bnd', out, Wout)
        mu = jnp.mean(out, axis=-1, keepdims=True)
        var = jnp.var(out, axis=-1, keepdims=True)
        out = (out - mu) * jax.lax.rsqrt(var + EPS) * ln_scale + ln_bias
        return out

    def _L0_ffn_ref(x, w_gate, w_up, w_down):
        import jax, jax.numpy as jnp
        import numpy as np
        BLOCK = 32
        W_BITS = 4
        ACT_BITS = 16

        def act_qdq(x):
            qmax = 2.0 ** (ACT_BITS - 1) - 1.0
            scale = jnp.maximum(jnp.max(jnp.abs(x)) / qmax, 1e-12)
            return jnp.clip(jnp.round(x / scale), -qmax - 1.0, qmax) * scale

        def fixed_qdq_u16(x):
            scale = 1.0 / 65536.0
            return jnp.clip(jnp.round(x / scale), 0.0, 65535.0) * scale

        def lpbq_dequant(w):
            O, I = w.shape
            qmax = 2.0 ** (W_BITS - 1) - 1.0
            wb = w.reshape(O, I // BLOCK, BLOCK)
            s = jnp.maximum(jnp.max(jnp.abs(wb), axis=-1, keepdims=True) / qmax, 1e-12)
            wq = jnp.clip(jnp.round(wb / s), -qmax - 1.0, qmax) * s
            return wq.reshape(O, I)
        x = act_qdq(x)
        up = act_qdq(x @ lpbq_dequant(w_up).T)
        gate = act_qdq(x @ lpbq_dequant(w_gate).T)
        sig = fixed_qdq_u16(jax.nn.sigmoid(gate))
        gate = act_qdq(gate * sig)
        o = act_qdq(gate * up)
        return o @ lpbq_dequant(w_down).T
    x = x + jnp.tanh(g_xattn[0]) * _L0_xattn_ref(_layernorm(x, axis=-1), ctx_2048, L0_xattn_Wq, L0_xattn_Wkv, L0_xattn_null_kv, L0_xattn_Wout, L0_xattn_ln_scale, L0_xattn_ln_bias)
    x = x + jnp.tanh(g_ffn[0]) * _L0_ffn_ref(_layernorm(x, axis=-1), L0_ffn_w_gate, L0_ffn_w_up, L0_ffn_w_down)
    return x

_drawn_inputs = setup_inputs


def setup_inputs(seed=0):
    import zlib

    import numpy as np

    out = dict(_drawn_inputs(seed))
    spreads = {'L0_xattn_ln_scale': (1.0, 0.2), 'L0_xattn_ln_bias': (0.0, 0.1)}
    factors = {'L0_xattn_null_kv': 5.376}
    for name, (base, spread) in spreads.items():
        noise = np.random.default_rng([zlib.crc32(name.encode()), seed]).standard_normal(out[name].shape)
        drawn = base * np.exp(spread * noise) if base else spread * noise
        out[name] = jnp.asarray(drawn.astype(out[name].dtype))
    for name, factor in factors.items():
        out[name] = (out[name] * factor).astype(out[name].dtype)
    return out
```

```python
from contextlib import ExitStack

import concourse.bass as bass
from concourse import mybir

ALU = mybir.AluOpType
ACT = mybir.ActivationFunctionType
AX = mybir.AxisListType
F32 = mybir.dt.float32
F32R = mybir.dt.float32r
I16 = mybir.dt.int16
U16 = mybir.dt.uint16
I32 = mybir.dt.int32

P = 128
EPS_LN = 1e-5
EPS_OUT = 1e-6
QMAX = 32767.0
WMAX = 7.0
WBLOCK = 32
MIN_SCALE = 1e-12
RSQRT_MAGIC = 1597463007.0
NEWTON = 3

TERMS = ((0, 0), (0, 1), (1, 0))


def wait(engine, sem, value):
    if not isinstance(value, int) or value > 0:
        engine.wait_ge(sem, value)


class Chain:

    def __init__(self, engine, sem, per):
        self.engine, self.sem, self.per = engine, sem, per

    def start(self, call):
        self.base, self.k = call * self.per, 0

    def link(self, ins):
        self.k += 1
        ins.then_inc(self.sem, 1)
        self.engine.wait_ge(self.sem, self.base + self.k)

    def end(self):
        assert self.k == self.per, (self.k, self.per)


def gated_cross_attention_ffn(nc, x, ctx, g_xattn, g_ffn, Wq, Wkv, null_kv, Wout, ln_scale, ln_bias,
                              w_gate, w_up, w_down, out):
    B, S, D = x.shape
    C = ctx.shape[2]
    INNER = Wq.shape[1]
    DH = null_kv.shape[1]
    HEADS = INNER // DH
    I = w_gate.shape[0]
    GB = 2
    NG = B // GB
    TG = GB * S
    KD, KC, KF = D // P, C // P, INNER // P
    NS = KF
    KI = I // P
    NT = B * S // P
    QW = S + 2
    NK = S + 1
    VW = 3 * DH
    SCALE = float(DH) ** -0.5

    PRO = ["X", "Ca", "Cb"] + [f"Q{c}" for c in range(NS)] + ["V00", "V10", "V01", "V11", "X", "Ca", "Cb", "W"]
    BODY = ["Q0", "Q1", "Q2", "Q3", "Q4", "Q5", "V00", "Q6", "V10", "Q7", "V01", "V11", "X", "Ca", "Cb", "W"]
    PENULT = [u for u in BODY if u not in ("X", "Ca", "Cb")]
    FINAL = [f"F{i}" for i in range(9)] + ["W"]
    LOOPED = NG - 2

    def units(g):
        if isinstance(g, str):
            return PRO, 0, 0
        if isinstance(g, int) and g == NG - 1:
            n = LOOPED * len(BODY) + len(PENULT)
            return FINAL, len(PRO) + n, len(PRO) - 1 + n - (NG - 1)
        seq = PENULT if isinstance(g, int) and g == LOOPED else BODY
        return seq, g * len(BODY) + len(PRO), g * (len(BODY) - 1) + len(PRO) - 1

    def parity(g, pos):
        if isinstance(g, str) or isinstance(g, int):
            return (units(g)[1] + pos) % 2
        return (len(PRO) + pos) % 2

    def feeds(g):
        return not isinstance(g, int) or g < LOOPED

    x_t = x.rearrange("b s d -> s b d")
    ctx_t = ctx.rearrange("b s d -> s b d")
    out_t = out.rearrange("b s d -> s b d")
    x2_dram = nc.dram_tensor("x2_scratch", (B, S, D), F32, kind="Internal").ap()
    x2_t = x2_dram.rearrange("b s d -> s b d")

    keep, att, ffn = ExitStack(), ExitStack(), ExitStack()
    with keep:
        stack = [keep]

        def sb(name, shape, dt=F32):
            return stack[0].enter_context(nc.sbuf_tensor(name, shape, dt))

        def sem(name):
            return keep.enter_context(nc.semaphore(name))

        ident = sb("ident", [P, P])
        ones = sb("ones", [1, P])
        gates = sb("gates", [P, 2])
        mean_var = sb("mean_var", [P, NT, 2])
        x2_max = sb("x2_max", [P, NT])
        x2_min = sb("x2_min", [P, NT])
        pause = sb("pause", [P, 1])
        small = sb("small", [P, 64])

        stack[0] = att
        wkv = [sb(f"wkv{i}", [P, KC, 2 * INNER], F32R) for i in range(2)]
        wq = [sb(f"wq{i}", [P, KD, INNER], F32R) for i in range(2)]
        wout = [sb(f"wout{i}", [P, KF, D], F32R) for i in range(2)]
        qk = [sb(f"qk{i}", [P, NS, 2 * GB, QW], F32R) for i in range(2)]
        v = [sb(f"v{i}", [P, GB, NS, VW], F32R) for i in range(2)]
        xnT = [sb(f"xnT{i}", [P, KD, TG], F32R) for i in range(2)]
        ctxT = [sb(f"ctxT{i}", [P, KC, TG], F32R) for i in range(2)]
        wnull = [sb(f"wnull{i}", [HEADS, D], F32R) for i in range(2)]
        nullT = [sb(f"nullT{i}", [HEADS, TG], F32R) for i in range(2)]
        gs = sb("gs", [P, D])
        gb = sb("gb", [P, D])
        nmax = sb("nmax", [P, 2, 4])
        rowsum = sb("rowsum", [P, 2, 4])
        rinv = sb("rinv", [P, 2, 4])
        pnull = sb("pnull", [P, GB, HEADS])
        bn = sb("bn", [P, 4, 6])
        mv = sb("mv", [P, 4, 2])
        rs = sb("rs", [P, 8, 2])
        xa = sb("xa", [P, GB, D])
        xr = sb("xr", [P, GB, D])
        y = sb("y", [P, GB, D])
        craw = sb("craw", [P, GB, C])
        late = ExitStack()
        stack[0] = late
        probs = sb("probs", [P, 2, 4, QW])
        pT = [sb(f"pT{i}", [P, 4, P], F32R) for i in range(2)]
        oT = [sb(f"oT{i}", [P, KF, TG], F32R) for i in range(2)]
        late.close()
        stack[0] = late = ExitStack()
        NST = 4
        STW = 1024
        stage = sb("stage", [P, NST, STW])
        nkw = sb("nkw", [P, NS * GB, 2])
        nvm = sb("nvm", [P, KF, HEADS])
        nvr = [sb(f"nvr{i}", [P, KF, HEADS], F32R) for i in range(2)]
        ncol = sb("ncol", [P, 2])
        late.close()
        att.close()

        stack[0] = ffn
        wg = [sb(f"wg{i}", [P, KD, I], F32R) for i in range(2)]
        wu = [sb(f"wu{i}", [P, KD, I], F32R) for i in range(2)]
        wd = [sb(f"wd{i}", [P, KI, D], F32R) for i in range(2)]
        NBK = I * D // P // WBLOCK
        early = ExitStack()
        stack[0] = early
        x2all = sb("x2all", [P, NT, D])
        fraw = sb("fraw", [P, NBK, WBLOCK])
        fint = sb("fint", [P, NBK, WBLOCK], I16)
        fs = sb("fs", [P, 2, NBK])
        early.close()
        stack[0] = ffn
        up = sb("up", [P, KI, B * S])
        xT = [sb(f"xT{i}", [P, KD, B * S], F32R) for i in range(2)]
        early = ExitStack()
        stack[0] = early
        gate = sb("gate", [P, KI, B * S])
        early.close()
        early = ExitStack()
        stack[0] = early
        oI = [sb(f"oI{i}", [P, 2, KI, 512], F32R) for i in range(2)]
        early.close()
        early = ExitStack()
        stack[0] = ffn
        gate_pad = sb("gate_pad", [P, KI, B * S])
        CH = 1024
        NCH = KI * B * S // CH
        tgi = sb("tgi", [P, 2, CH], I16)
        tsg = sb("tsg", [P, 2, CH])
        tsi = sb("tsi", [P, 2, CH], U16)
        tpi = sb("tpi", [P, 2, CH], I16)
        tui = sb("tui", [P, 2, CH], I16)
        xi = sb("xi", [P, 2, 2, D], I16)
        xf = sb("xf", [P, 2, 2, D])
        xres = sb("xres", [P, 2, 2, D])
        yout = sb("yout", [P, 2, 2, D])
        fa = sb("fa", [P, 4, NT])
        rs3 = sb("rs3", [P, 4, NT])
        amax = sb("amax", [P, 4, 24])
        ffn.close()

        bank = [keep.enter_context(nc.psum_tensor(f"bank{i}", [P, 512], F32)) for i in range(8)]
        score_bank = [[bank[0], bank[1]], [bank[2], bank[3]]]
        pt_bank, pv_bank = bank[4], bank[5]
        unit_bank = [bank[6], bank[7]]

        stage_in = [sem(f"stage_in{i}") for i in range(NST)]
        wsplit_hi, wsplit_lo = sem("wsplit_hi"), sem("wsplit_lo")
        const_in, const_ready, null_ready = sem("const_in"), sem("const_ready"), sem("null_ready")
        ident_ready, ident_zero, vzero = sem("ident_ready"), sem("ident_zero"), sem("vzero")
        tanh_done = sem("tanh_done")
        x_in, ctx_in, xres_in, x2_out = sem("x_in"), sem("ctx_in"), sem("xres_in"), sem("x2_out")
        xn_ready = sem("xn_ready")
        unit_done, unit_hi, unit_lo, w_free = sem("unit_done"), sem("unit_hi"), sem("unit_lo"), sem("w_free")
        scores_done, max_done, exp_done = sem("scores_done"), sem("max_done"), sem("exp_done")
        rinv_done, norm_done, pnull_done = sem("rinv_done"), sem("norm_done"), sem("pnull_done")
        pt_done, pt_hi, pt_lo = sem("pt_done"), sem("pt_hi"), sem("pt_lo")
        pv_done, ot_hi, ot_lo = sem("pv_done"), sem("ot_hi"), sem("ot_lo")
        ln1_chain, ln2_chain, prep_chain = sem("ln1_chain"), sem("ln2_chain"), sem("prep_chain")
        xgb_ready, x2_ready, x2_read = sem("xgb_ready"), sem("x2_ready"), sem("x2_read")
        fraw_in, fscale, fint_ready, fw_ready = sem("fraw_in"), sem("fscale"), sem("fint_ready"), sem("fw_ready")
        x2all_in = sem("x2all_in")
        fchain, gm_t, gm_1, gm_b = sem("fchain"), sem("gm_t"), sem("gm_1"), sem("gm_b")
        scale_ready = sem("scale_ready")
        xi_ready, xf_ready, xt_done, xt_hi, xt_lo = (sem("xi_ready"), sem("xf_ready"), sem("xt_done"),
                                                     sem("xt_hi"), sem("xt_lo"))
        gu_done, gu_out, gu_max = sem("gu_done"), sem("gu_out"), sem("gu_max")
        gi_ready, sg_ready, si_ready, p_ready, pi_ready = (sem("gi_ready"), sem("sg_ready"), sem("si_ready"),
                                                           sem("p_ready"), sem("pi_ready"))
        ui_ready, o_ready, oi_ready, oh_ready, ol_ready = (sem("ui_ready"), sem("o_ready"), sem("oi_ready"),
                                                           sem("oh_ready"), sem("ol_ready"))
        down_done, y_ready = sem("down_done"), sem("y_ready")
        xres_ld = [sem(f"xres_ld{i}") for i in range(2)]
        y_out = [sem(f"y_out{i}") for i in range(2)]

        block = keep.enter_context(nc.Block())

        wq_r = Wq.rearrange("(k p) f -> p k f", p=P)
        wkv_r = Wkv.rearrange("(k p) f -> p k f", p=P)
        wout_r = Wout.rearrange("(k p) f -> p k f", p=P)
        pieces = [([w[:, k, :] for w in wq], wq_r[:, k, :], SCALE, None) for k in range(KD)]
        pieces += [([w[:, k, 0:INNER] for w in wkv], wkv_r[:, k, 0:INNER], 1.0, None) for k in range(KC)]
        pieces += [([w[:, k, INNER:] for w in wkv], wkv_r[:, k, INNER:], 1.0, None) for k in range(KC)]
        pieces += [([w[:, 4 * j:4 * j + 4, :] for w in wout], wout_r[:, 4 * j:4 * j + 4, :], 1.0, 4) for j in range(2)]
        NPC = len(pieces)
        READY_Q, READY_K, READY_V = KD, KD + KC, KD + 2 * KC

        def stage_view(i, fold):
            s = stage[:, i % NST, :]
            return s if fold is None else s.rearrange("p (a b) -> p a b", a=fold)

        fw_r = [w_gate.rearrange("(j p) h -> p j h", p=P), w_up.rearrange("(j p) h -> p j h", p=P), w_down.rearrange("(j p) i -> p j i", p=P)]

        def unit_view(kind, hl):
            if kind[0] == "Q":
                return qk[hl][:, int(kind[1]), :, 0:S]
            if kind[0] == "V":
                b, h = int(kind[1]), int(kind[2])
                return v[hl][:, b, 4 * h:4 * h + 4, :].rearrange("p c (a d) -> p c a d", d=DH)[:, :, 0:3:2, :]
            if kind == "X":
                return xnT[hl][:, :, :]
            if kind[0] == "C":
                b = "ab".index(kind[1])
                return ctxT[hl][:, :, b * S:(b + 1) * S]
            i = int(kind[1])
            m, r = i // 3, i % 3
            if m < 2:
                return (wg, wu)[m][hl][:, :, 2 * r * P:(2 * r + 2) * P]
            return wd[hl][:, 2 * r:2 * r + 2, :]

        def unit_psum(kind, bk):
            if kind[0] == "Q":
                return bk[:, :].rearrange("p (a s) -> p a s", s=S)
            if kind[0] == "V":
                return bk[:, :].rearrange("p (c a d) -> p c a d", a=2, d=DH)
            if kind[0] == "C":
                return bk[:, :].rearrange("p (a s) -> p a s", s=S)
            return bk[:, :].rearrange("p (a s) -> p a s", s=2 * P)

        @block.sync
        def _(sp):
            sp.dma_start(xa[:, :, :], x_t[:, 0:GB, :]).then_inc(x_in, 16)
            sp.dma_start(craw[:, :, :], ctx_t[:, 0:GB, :]).then_inc(ctx_in, 16)
            for i, (_, src, _, fold) in enumerate(pieces):
                if i >= NST:
                    sp.wait_ge(wsplit_lo, i - NST + 1)
                sp.dma_start(stage_view(i, fold), src).then_inc(stage_in[i % NST], 16)
                if i == 6:
                    sp.wait_ge(unit_done, 1)
                    sp.dma_start(xa[:, :, :], x_t[:, GB:2 * GB, :]).then_inc(x_in, 16)
                if i == 7:
                    sp.wait_ge(unit_done, 3)
                    sp.dma_start(craw[:, :, :], ctx_t[:, GB:2 * GB, :]).then_inc(ctx_in, 16)

            def group_loads(g):
                if feeds(g):
                    sp.wait_ge(unit_done, g * len(BODY) + len(PRO) - 3)
                    sp.dma_start(xa[:, :, :], x_t[:, bass.ds((g + 2) * GB, GB), :]).then_inc(x_in, 16)
                    sp.wait_ge(unit_done, g * len(BODY) + len(PRO) - 1)
                    sp.dma_start(craw[:, :, :], ctx_t[:, bass.ds((g + 2) * GB, GB), :]).then_inc(ctx_in, 16)
                wait(sp, x2_read, g)
                sp.dma_start(xr[:, :, :], x_t[:, bass.ds(g * GB, GB), :]).then_inc(xres_in, 16)

            def group_store(g):
                sp.wait_ge(x2_ready, g + 1)
                src = x2all[:, g * GB:(g + 1) * GB, :] if isinstance(g, int) and g == NG - 1 else y[:, :, :]
                sp.dma_start(x2_t[:, bass.ds(g * GB, GB), :], src).then_inc(x2_out, 16)

            group_loads(0)
            group_store(0)
            with sp.Fori(1, LOOPED) as g:
                group_loads(g)
                group_store(g)
            group_loads(NG - 2)
            group_store(NG - 2)
            group_loads(NG - 1)
            sp.wait_ge(unit_done, units(NG - 1)[1])
            for m in range(3):
                if m:
                    sp.wait_ge(fw_ready, m)
                    sp.wait_ge(unit_done, units(NG - 1)[1] + 3 * m)
                sp.dma_start(fraw[:, :, :].rearrange("p n w -> p (n w)").rearrange(
                    "p (j h) -> p j h", j=(KI, KI, 2)[m]), fw_r[m]).then_inc(fraw_in, 16)
            sp.wait_ge(x2_out, 16 * (NG - 1))
            sp.dma_start(x2all[:, 0:(NG - 1) * GB, :], x2_t[:, 0:(NG - 1) * GB, :]).then_inc(x2all_in, 16)
            group_store(NG - 1)
            sp.wait_ge(x2_out, 16 * NG)
            sp.wait_ge(xi_ready, NT // 2)

            def load_residual(t):
                sp.dma_start(xres[:, t % 2, :, :], x2_t[:, 2 * t:2 * t + 2, :]).then_inc(xres_ld[t % 2], 16)

            load_residual(0)
            load_residual(1)
            for t in range(NT // 2):
                sp.wait_ge(y_ready, t + 1)
                sp.dma_start(out_t[:, 2 * t:2 * t + 2, :], yout[:, t % 2, :, :]).then_inc(y_out[t % 2], 16)
                if t + 2 < NT // 2:
                    load_residual(t + 2)
            for i in range(2):
                sp.wait_ge(y_out[i], 16 * (NT // 4))

        @block.tensor
        def _(pe):
            mm = nc.tensor.matmul

            def unit(g, pos):
                seq, first, split_first = units(g)
                kind, bk = seq[pos], unit_bank[parity(g, pos)]
                if pos >= 2:
                    pe.wait_ge(unit_lo, split_first + pos - 1)
                elif not isinstance(g, str):
                    if pos == 0:
                        pe.wait_ge(unit_lo, split_first)
                    else:
                        pe.wait_ge(w_free, g + 1)
                if kind[0] == "Q":
                    c = int(kind[1])
                    if isinstance(g, str) and c == 0:
                        pe.wait_ge(unit_lo, 3)
                        pe.wait_ge(wsplit_lo, READY_K)
                    elif c == 0:
                        pe.wait_ge(unit_lo, split_first)
                    f = slice(c * P, (c + 1) * P)
                    for n, (wt, act_t, kk) in enumerate(((wq, xnT, KD), (wkv, ctxT, KC))):
                        for k in range(kk):
                            for i, (a, b) in enumerate(TERMS):
                                last = mm(bk[:, n * TG:(n + 1) * TG], wt[a][:, k, f], act_t[b][:, k, :],
                                          start=(k == 0 and i == 0), stop=(k == kk - 1 and i == len(TERMS) - 1))
                elif kind[0] == "V":
                    b, h = int(kind[1]), int(kind[2])
                    if isinstance(g, str) and pos == PRO.index("V00"):
                        pe.wait_ge(wsplit_lo, READY_V)
                    for k in range(KC):
                        for i, (a, w) in enumerate(TERMS):
                            last = mm(bk[:, :], ctxT[a][:, k, b * S:(b + 1) * S],
                                      wkv[w][:, k, INNER + h * 512:INNER + (h + 1) * 512],
                                      start=(k == 0 and i == 0), stop=(k == KC - 1 and i == len(TERMS) - 1))
                elif kind == "X":
                    n = (0 if pos == 0 else 1) if isinstance(g, str) else g + 2
                    if isinstance(g, str) and pos == 0:
                        pe.wait_ge(ident_ready, 1)
                    pe.wait_ge(xn_ready, n + 1)
                    for k in range(KD):
                        for b in range(GB):
                            last = nc.tensor.transpose(bk[:, k * TG + b * S:k * TG + (b + 1) * S],
                                                       xa[:, b, k * P:(k + 1) * P], ident[:, :])
                elif kind[0] == "C":
                    b = "ab".index(kind[1])
                    n = (0 if pos < 3 else 1) if isinstance(g, str) else g + 2
                    if b == 0:
                        pe.wait_ge(ctx_in, (n + 1) * 16)
                    for k in range(KC):
                        last = nc.tensor.transpose(bk[:, k * S:(k + 1) * S], craw[:, b, k * P:(k + 1) * P],
                                                   ident[:, :])
                elif kind[0] == "F":
                    i = int(kind[1])
                    m, r = i // 3, i % 3
                    if r == 0:
                        pe.wait_ge(fw_ready, m + 1)
                    wf = fraw[:, :, :].rearrange("p n w -> p (n w)")
                    for a in range(2):
                        for b in range(2):
                            src = ((2 * r + b) * D + a * P) if m < 2 else (b * I + (2 * r + a) * P)
                            last = nc.tensor.transpose(bk[:, (2 * a + b) * P:(2 * a + b + 1) * P],
                                                       wf[:, src:src + P], ident[:, :])
                elif isinstance(g, str):
                    pe.wait_ge(null_ready, 2)
                    pe.wait_ge(wsplit_lo, NPC)
                    for k in range(KF):
                        for i, (a, w) in enumerate(TERMS):
                            last = mm(bk[0:HEADS, 0:D], nvr[a][:, k, :], wout[w][:, k, :],
                                      start=(k == 0 and i == 0), stop=(k == KF - 1 and i == len(TERMS) - 1))
                else:
                    wait(pe, ot_lo, g * NS + NS)
                    wait(pe, pt_lo, g * (NS + 1) + NS + 1)
                    pe.wait_ge(w_free, g + 1)
                    for b in range(GB):
                        o = bk[:, b * D:(b + 1) * D]
                        for k in range(KF):
                            for i, (a, w) in enumerate(TERMS):
                                mm(o, oT[a][:, k, b * S:(b + 1) * S], wout[w][:, k, :],
                                   start=(k == 0 and i == 0), stop=False)
                        for i, (a, w) in enumerate(TERMS):
                            last = mm(o, nullT[a][:, b * S:(b + 1) * S], wnull[w][:, :],
                                      start=False, stop=(i == len(TERMS) - 1))
                last.then_inc(unit_done, 1)

            def scores(g, c):
                wait(pe, exp_done, g * NS + c - 1)
                for b in range(GB):
                    for i, (a, w) in enumerate(TERMS):
                        for h in range(2):
                            rows = slice(h * DH, (h + 1) * DH)
                            last = mm(score_bank[c % 2][h][:, b * QW:(b + 1) * QW], qk[a][rows, c, b, 0:S],
                                      qk[w][rows, c, GB + b, 0:QW], start=(i == 0), stop=(i == len(TERMS) - 1))
                last.then_inc(scores_done, 1)

            def prob_transposes(g, c):
                pe.wait_ge(norm_done, g * NS + c + 1)
                wait(pe, pt_lo, g * (NS + 1) + c)
                for u in range(4):
                    last = nc.tensor.transpose(pt_bank[:, u * P:(u + 1) * P], probs[:, c % 2, u, 0:S], ident[:, :])
                last.then_inc(pt_done, 1)

            def null_transposes(g):
                wait(pe, pnull_done, g * NS + NS)
                wait(pe, pt_lo, g * (NS + 1) + NS)
                for b in range(GB):
                    last = nc.tensor.transpose(pt_bank[0:HEADS, b * S:(b + 1) * S], pnull[:, b, :], ident[:, :])
                last.then_inc(pt_done, 1)

            def values(g, c):
                wait(pe, pt_lo, g * (NS + 1) + c + 1)
                wait(pe, ot_lo, g * NS + c)
                for b in range(GB):
                    n = 0
                    for h in range(2):
                        for a, w in TERMS:
                            last = mm(pv_bank[:, b * S:(b + 1) * S], v[a][:, b, c, h * DH:h * DH + P],
                                      pT[w][:, 2 * h + b, :], start=(n == 0), stop=(n == 5))
                            n += 1
                last.then_inc(pv_done, 1)

            for pos in range(len(PRO)):
                unit("pro", pos)
                if PRO[pos] == "Q7":
                    pe.wait_ge(null_ready, 1)
                    scores(0, 0)

            def group(g):
                final = isinstance(g, int) and g == NG - 1
                pos = 0
                seq = units(g)[0]
                for c in range(NS):
                    if c + 1 < NS:
                        scores(g, c + 1)
                    todo = [seq[pos]] if final else [s for s in (f"Q{c}", {5: "V00", 6: "V10"}.get(c)) if s]
                    for s in todo:
                        assert seq[pos] == s
                        unit(g, pos)
                        pos += 1
                    prob_transposes(g, c)
                    if c:
                        values(g, c - 1)
                if not final:
                    scores(g + 1, 0)
                values(g, NS - 1)
                while pos < len(seq):
                    if seq[pos] in ("X", "W") and (seq[pos] == "X" or "X" not in seq):
                        null_transposes(g)
                    unit(g, pos)
                    pos += 1

            pe.wait_ge(vzero, 1)
            group(0)
            with pe.Fori(1, LOOPED) as g:
                group(g)
            group(NG - 2)
            group(NG - 1)

            def global_max(n):
                pe.wait_ge(gm_t, 2 * n + 1)
                nc.tensor.transpose(bank[0][0:1, 0:P], small[:, 0:1], ident[:, :]).then_inc(gm_1, 1)
                pe.wait_ge(gm_t, 2 * n + 2)
                mm(bank[1][:, 0:1], ones[:, :], small[0:1, 1:2], start=True, stop=True).then_inc(gm_b, 1)

            global_max(0)
            for t in range(NT // 2):
                pe.wait_ge(xf_ready, t + 1)
                if t >= 2:
                    pe.wait_ge(xt_lo, t - 1)
                for k in range(KD):
                    for b in range(2):
                        last = nc.tensor.transpose(unit_bank[t % 2][:, (2 * k + b) * P:(2 * k + b + 1) * P],
                                                   xf[:, t % 2, b, k * P:(k + 1) * P], ident[:, :])
                last.then_inc(xt_done, 1)

            for m in range(2):
                for tg in range(4):
                    for j in range(KI):
                        n = (m * 4 + tg) * KI + j
                        if m == 0 and j == 0:
                            pe.wait_ge(xt_lo, 2 * tg + 2)
                        bk = bank[2 + n % 4]
                        if n >= 4:
                            pe.wait_ge(gu_out, n - 3)
                        for k in range(KD):
                            for i, (a, w) in enumerate(TERMS):
                                last = mm(bk[:, :], (wg, wu)[m][a][:, k, j * P:(j + 1) * P],
                                          xT[w][:, k, tg * 512:(tg + 1) * 512],
                                          start=(k == 0 and i == 0), stop=(k == KD - 1 and i == len(TERMS) - 1))
                        last.then_inc(gu_done, 1)
                        if m == 1 and tg == 0 and j == 3:
                            global_max(1)
            for n in range(2, 5):
                global_max(n)
            for t in range(NT):
                tg = t // 4
                if t % 4 == 0:
                    pe.wait_ge(ol_ready, (tg + 1) * KI)
                bk = bank[2 + (t // 2) % 4]
                if t % 2 == 0 and t >= 8:
                    pe.wait_ge(y_ready, t // 2 - 3)
                for j in range(KI):
                    for i, (a, w) in enumerate(TERMS):
                        last = mm(bk[:, (t % 2) * D:(t % 2 + 1) * D], oI[a][:, tg % 2, j, (t % 4) * P:(t % 4 + 1) * P],
                                  wd[w][:, j, :], start=(j == 0 and i == 0), stop=(j == KI - 1 and i == 2))
                last.then_inc(down_done, 1)

        @block.scalar
        def _(act):
            act_copy = ACT.Copy

            def high(dst, src, scale=1.0):
                return nc.scalar.activation(dst, src, act_copy, scale=scale)

            act.wait_ge(const_in, 16 * 6)
            nc.scalar.activation(gates[:, :], gates[:, :], ACT.Tanh).then_inc(tanh_done, 1)

            def split(g, pos):
                seq, first, _ = units(g)
                kind = seq[pos]
                if kind == "W":
                    if isinstance(g, str):
                        act.wait_ge(unit_done, first + pos + 1)
                        high(wnull[0][:, :], unit_bank[parity(g, pos)][0:HEADS, 0:D]).then_inc(unit_hi, 1)
                    return
                act.wait_ge(unit_done, first + pos + 1)
                high(unit_view(kind, 0), unit_psum(kind, unit_bank[parity(g, pos)])).then_inc(unit_hi, 1)

            def exps(g, c):
                act.wait_ge(max_done, g * NS + c + 1)
                if not (isinstance(g, int) and g == 0 and c < 2):
                    if c == 0:
                        wait(act, pt_done, g * (NS + 1) - 2)
                    else:
                        wait(act, pt_done, g * (NS + 1) + (c - 1 if c > 1 else 0))
                    wait(act, pnull_done, g * NS + c - 1)
                for u in range(4):
                    h, b = u // 2, u % 2
                    last = nc.scalar.activation(probs[:, c % 2, u, 0:NK],
                                                score_bank[c % 2][h][:, b * QW:b * QW + NK], ACT.Exp,
                                                bias=nmax[:, c % 2, u:u + 1], accum_out=rowsum[:, c % 2, u:u + 1])
                last.then_inc(exp_done, 1)

            def prob_high(g, c):
                wait(act, pt_done, g * (NS + 1) + c + 1)
                wait(act, pv_done, g * NS + c)
                high(pT[0][:, :, :], pt_bank[:, :].rearrange("p (u s) -> p u s", u=4)).then_inc(pt_hi, 1)

            def out_high(g, c):
                wait(act, pv_done, g * NS + c + 1)
                high(oT[0][:, c, :], pv_bank[:, 0:TG]).then_inc(ot_hi, 1)

            npos = [0]
            for i, (dst, _, f, fold) in enumerate(pieces):
                if i in (READY_Q, READY_K - 1):
                    for _ in range(2 if i == READY_Q else 1):
                        split("pro", npos[0])
                        npos[0] += 1
                act.wait_ge(stage_in[i % NST], 16 * (i // NST + 1))
                high(dst[0], stage_view(i, fold), f).then_inc(wsplit_hi, 1)
                if i >= READY_K and PRO[npos[0]] != "V00":
                    split("pro", npos[0])
                    npos[0] += 1
            while npos[0] < len(PRO):
                split("pro", npos[0])
                if PRO[npos[0]] == "Q7":
                    exps(0, 0)
                npos[0] += 1

            def group(g):
                final = isinstance(g, int) and g == NG - 1
                seq, pos = units(g)[0], 0
                for c in range(NS):
                    if c + 1 < NS:
                        exps(g, c + 1)
                    for s in ([0] if final else [s for s in (f"Q{c}", {5: "V00", 6: "V10"}.get(c)) if s]):
                        split(g, pos)
                        pos += 1
                    prob_high(g, c)
                    if c:
                        out_high(g, c - 1)
                if not final:
                    exps(g + 1, 0)
                out_high(g, NS - 1)
                while pos < len(seq):
                    if seq[pos] in ("X", "W") and (seq[pos] == "X" or "X" not in seq):
                        wait(act, pt_done, g * (NS + 1) + NS + 1)
                        high(nullT[0][:, :], pt_bank[0:HEADS, 0:TG]).then_inc(pt_hi, 1)
                    split(g, pos)
                    pos += 1

            group(0)
            with act.Fori(1, LOOPED) as g:
                group(g)
            group(NG - 2)
            group(NG - 1)

            for t in range(NT // 2):
                act.wait_ge(xi_ready, t + 1)
                if t >= 2:
                    act.wait_ge(xt_done, t - 1)
                high(xf[:, t % 2, :, :], xi[:, t % 2, :, :]).then_inc(xf_ready, 1)
                if t >= 1:
                    act.wait_ge(xt_done, t)
                    high(xT[0][:, :, (t - 1) * TG:t * TG],
                         unit_bank[(t - 1) % 2][:, :].rearrange("p (k s) -> p k s", k=KD)).then_inc(xt_hi, 1)
            t = NT // 2
            act.wait_ge(xt_done, t)
            high(xT[0][:, :, (t - 1) * TG:t * TG],
                 unit_bank[(t - 1) % 2][:, :].rearrange("p (k s) -> p k s", k=KD)).then_inc(xt_hi, 1)

            def gu(m, n):
                tg, j = n // KI, n % KI
                q = m * 4 * KI + n
                act.wait_ge(gu_done, q + 1)
                nc.scalar.activation((gate, up)[m][:, j, tg * 512:(tg + 1) * 512], bank[2 + q % 4][:, :],
                                     act_copy).then_inc(gu_out, 1)

            for n in range(4 * KI):
                gu(0, n)
            gate_c = gate[:, :, :].rearrange("p j t -> p (j t)")
            up_c = up[:, :, :].rearrange("p j t -> p (j t)")
            act.wait_ge(x2_out, 16 * NG)
            for q in range(NCH):
                gu(1, 2 * q)
                gu(1, 2 * q + 1)
                act.wait_ge(gi_ready, q + 1)
                if q >= 2:
                    act.wait_ge(si_ready, q - 1)
                nc.scalar.activation(tsg[:, q % 2, :], tgi[:, q % 2, :], ACT.Sigmoid,
                                     scale=small[:, 10:11]).then_inc(sg_ready, 1)
            for q in range(NCH):
                if q == 0:
                    act.wait_ge(scale_ready, 2)
                if q >= 2:
                    act.wait_ge(o_ready, q - 1)
                nc.scalar.activation(tui[:, q % 2, :], up_c[:, q * CH:(q + 1) * CH], act_copy,
                                     scale=small[:, 12:13]).then_inc(ui_ready, 1)
            for n in range(4 * KI):
                act.wait_ge(oi_ready, n + 1)
                tg, j = n // KI, n % KI
                if tg >= 2 and j == 0:
                    act.wait_ge(down_done, 4 * (tg - 1))
                high(oI[0][:, tg % 2, j, :], tgi[:, n % 2, 0:512]).then_inc(oh_ready, 1)

        @block.vector
        def _(dve):
            V = nc.vector

            def low(dst, src, hi, f=1.0):
                if f == 1.0:
                    return V.tensor_tensor(dst, src, hi.bitcast(F32), ALU.subtract)
                return V.scalar_tensor_tensor(out=dst, in0=src, scalar=f, in1=hi.bitcast(F32), op0=ALU.mult,
                                              op1=ALU.subtract)

            def rsqrt(link, var, r, eps):
                link(V.tensor_scalar(r[1], var, eps, None, ALU.add))
                link(V.tensor_scalar(r[0].bitcast(I32), r[1].bitcast(I32), -0.5, RSQRT_MAGIC, ALU.mult, ALU.add))
                for _ in range(NEWTON):
                    link(V.scalar_tensor_tensor(out=r[2], in0=r[0], scalar=-0.5, in1=r[0],
                                                      op0=ALU.mult, op1=ALU.mult))
                    link(V.tensor_tensor(r[2], r[2], r[1], ALU.mult))
                    link(V.scalar_tensor_tensor(out=r[0], in0=r[2], scalar=1.5, in1=r[0],
                                                      op0=ALU.add, op1=ALU.mult))

            def settle():
                V.memset(pause[:, :], 0.0)

            NRS = 2 + 3 * NEWTON
            ln1 = Chain(dve, ln1_chain, 2 + NRS)
            ln2 = Chain(dve, ln2_chain, 2 + NRS + 5)

            def ln_input(n):
                dve.wait_ge(x_in, (n + 1) * 16)
                ln1.start(n)
                for b in range(GB):
                    last = V.bn_stats(bn[:, b, :], xa[:, b, :])
                ln1.link(last)
                settle()
                for b in range(GB):
                    last = V.bn_aggr(mv[:, b, :], bn[:, b, :])
                ln1.link(last)
                rsqrt(ln1.link, mv[:, 0:2, 1], [rs[:, i, :] for i in range(3)], EPS_LN)
                ln1.end()
                for b in range(GB):
                    last = V.tensor_scalar(xa[:, b, :], xa[:, b, :], mv[:, b, 0:1], rs[:, 0, b:b + 1],
                                           ALU.subtract, ALU.mult)
                last.then_inc(xn_ready, 1)

            def split(g, pos):
                seq, first, split_first = units(g)
                kind = seq[pos]
                bk = unit_bank[parity(g, pos)]
                if kind == "W":
                    if isinstance(g, str):
                        dve.wait_ge(unit_hi, split_first + pos + 1)
                        low(wnull[1][:, :], bk[0:HEADS, 0:D], wnull[0][:, :]).then_inc(w_free, 1)
                    else:
                        attention_out(g, bk, first + pos)
                    return
                n = split_first + pos + 1
                dve.wait_ge(unit_hi, n if isinstance(g, str) else n + 1)
                low(unit_view(kind, 1), unit_psum(kind, bk), unit_view(kind, 0)).then_inc(unit_lo, 1)

            def attention_out(g, bk, number):
                lastg = isinstance(g, int) and g == NG - 1
                dve.wait_ge(unit_done, number + 1)
                ln2.start(g)
                for b in range(GB):
                    last = V.bn_stats(bn[:, 2 + b, :], bk[:, b * D:(b + 1) * D])
                ln2.link(last)
                settle()
                for b in range(GB):
                    last = V.bn_aggr(mv[:, 2 + b, :], bn[:, 2 + b, :])
                ln2.link(last)
                rsqrt(ln2.link, mv[:, 2:4, 1], [rs[:, 4 + i, :] for i in range(3)], EPS_OUT)
                dst = x2all[:, g * GB:(g + 1) * GB, :] if lastg else y[:, :, :]
                dve.wait_ge(const_ready, 1)
                wait(dve, x2_out, g * 16)
                for b in range(GB):
                    last = V.tensor_scalar(dst[:, b, :], bk[:, b * D:(b + 1) * D], mv[:, 2 + b, 0:1],
                                           rs[:, 4, b:b + 1], ALU.subtract, ALU.mult)
                last.then_inc(w_free, 1)
                dve.wait_ge(w_free, g + 2)
                for b in range(GB):
                    last = V.tensor_tensor(dst[:, b, :], dst[:, b, :], gs[:, :], ALU.mult)
                ln2.link(last)
                dve.wait_ge(xgb_ready, g + 1)
                ln2.link(V.tensor_tensor(dst, dst, xr[:, :, :], ALU.add))
                for b in range(GB):
                    last = V.bn_stats(bn[:, 2 + b, :], dst[:, b, :])
                V.tensor_reduce(x2_max[:, bass.ds(g * GB, GB)], dst, AX.X, ALU.max).then_inc(x2_read, 1)
                V.tensor_reduce(x2_min[:, bass.ds(g * GB, GB)], dst, AX.X, ALU.min).then_inc(x2_ready, 1)
                ln2.link(last)
                settle()
                for b in range(GB):
                    last = V.bn_aggr(mv[:, 2 + b, :], bn[:, 2 + b, :])
                ln2.link(last)
                settle()
                ln2.link(V.tensor_copy(mean_var[:, bass.ds(g * GB, GB), :], mv[:, 2:4, :]))
                ln2.end()

            def maxima(g, c):
                dve.wait_ge(scores_done, g * NS + c + 1)
                for h in range(2):
                    last = V.tensor_reduce(nmax[:, c % 2, 2 * h:2 * h + 2],
                                           score_bank[c % 2][h][:, 0:GB * QW].rearrange(
                                               "p (b s) -> p b s", b=GB)[:, :, 0:NK],
                                           AX.X, ALU.max, negate=True)
                last.then_inc(max_done, 1)

            def inverse_sums(g, c):
                wait(dve, exp_done, g * NS + c + 1)
                V.reciprocal(rinv[:, c % 2, :], rowsum[:, c % 2, :]).then_inc(rinv_done, 1)

            def prob_low(g, c):
                dve.wait_ge(pt_hi, g * (NS + 1) + c + 1)
                low(pT[1][:, :, :], pt_bank[:, :].rearrange("p (u s) -> p u s", u=4), pT[0][:, :, :]).then_inc(pt_lo, 1)

            def out_low(g, c):
                dve.wait_ge(ot_hi, g * NS + c + 1)
                low(oT[1][:, c, :], pv_bank[:, 0:TG], oT[0][:, c, :]).then_inc(ot_lo, 1)

            V.memset(ones[:, :], 1.0)
            V.memset(nkw[:, :, :], 0.0).then_inc(prep_chain, 1)
            V.memset(nvm[:, :, :], 0.0).then_inc(prep_chain, 1)
            ln_input(0)
            npos = [0]

            def constants():
                dve.wait_ge(tanh_done, 1)
                dve.wait_ge(prep_chain, 2)
                V.tensor_scalar(gs[:, :], gs[:, :], gates[:, 0:1], None, ALU.mult)
                V.tensor_scalar(gb[:, :], gb[:, :], gates[:, 0:1], None, ALU.mult).then_inc(const_ready, 1)
                V.tensor_scalar(nkw[:, :, 0:1], nkw[:, :, 0:1], ncol[:, 0:1], None, ALU.add)
                diag = nvm[:, :, :].rearrange("p k h -> p (k h)")
                for h in range(2):
                    rows = slice(h * DH, (h + 1) * DH)
                    d = diag[rows, h:h + (HEADS + 2) * (KF - 1) + 1:HEADS + 2]
                    last = V.tensor_scalar(d, d, ncol[rows, 1:2], None, ALU.add)
                last.then_inc(prep_chain, 1)
                dve.wait_ge(prep_chain, 3)
                pad = [qk[i][:, :, GB:2 * GB, S:QW] for i in range(2)]
                nk4 = nkw[:, :, :].rearrange("p (c b) t -> p c b t", b=GB)
                V.tensor_copy(pad[0], nk4)
                V.tensor_copy(nvr[0][:, :, :], nvm[:, :, :]).then_inc(prep_chain, 1)
                dve.wait_ge(prep_chain, 4)
                low(pad[1], nk4, pad[0]).then_inc(null_ready, 1)
                low(nvr[1][:, :, :], nvm[:, :, :], nvr[0][:, :, :]).then_inc(null_ready, 1)

            for i, (dst, _, f, fold) in enumerate(pieces):
                if i in (READY_Q, READY_K - 1):
                    for _ in range(2 if i == READY_Q else 1):
                        split("pro", npos[0])
                        npos[0] += 1
                if i == READY_K - 1:
                    constants()
                dve.wait_ge(wsplit_hi, i + 1)
                low(dst[1], stage_view(i, fold), dst[0], f).then_inc(wsplit_lo, 1)
                if i >= READY_K and PRO[npos[0]] != "V00":
                    split("pro", npos[0])
                    npos[0] += 1
            while npos[0] < len(PRO):
                if PRO[npos[0]] == "V00":
                    ln_input(1)
                split("pro", npos[0])
                if PRO[npos[0]] == "Q7":
                    maxima(0, 0)
                    inverse_sums(0, 0)
                npos[0] += 1

            def group(g):
                final = isinstance(g, int) and g == NG - 1
                seq, pos = units(g)[0], 0
                for c in range(NS):
                    if c + 1 < NS:
                        maxima(g, c + 1)
                        inverse_sums(g, c + 1)
                    for s in ([0] if final else [s for s in (f"Q{c}", {5: "V00", 6: "V10"}.get(c)) if s]):
                        split(g, pos)
                        pos += 1
                    prob_low(g, c)
                    if c:
                        out_low(g, c - 1)
                    if c == 5 and feeds(g):
                        ln_input(g + 2)
                if not final:
                    maxima(g + 1, 0)
                    inverse_sums(g + 1, 0)
                out_low(g, NS - 1)
                while pos < len(seq):
                    if seq[pos] in ("X", "W") and (seq[pos] == "X" or "X" not in seq):
                        dve.wait_ge(pt_hi, g * (NS + 1) + NS + 1)
                        low(nullT[1][:, :], pt_bank[0:HEADS, 0:TG], nullT[0][:, :]).then_inc(pt_lo, 1)
                    split(g, pos)
                    pos += 1

            def weight_scales(m):
                dve.wait_ge(fraw_in, 16 * (m + 1))
                if m:
                    dve.wait_ge(fw_ready, m)
                V.tensor_reduce(fs[:, 0, :], fraw[:, :, :], AX.X, ALU.max, apply_absolute_value=True).then_inc(fchain, 1)
                dve.wait_ge(fchain, 3 * m + 1)
                V.tensor_scalar(fs[:, 0, :], fs[:, 0, :], 1.0 / WMAX, MIN_SCALE, ALU.mult, ALU.max).then_inc(fchain, 1)
                dve.wait_ge(fchain, 3 * m + 2)
                V.reciprocal(fs[:, 1, :], fs[:, 0, :]).then_inc(fchain, 1)
                dve.wait_ge(fchain, 3 * m + 3)
                bc = [fs[:, i, :].rearrange("p (n o) -> p n o", o=1).to_broadcast([P, NBK, WBLOCK]) for i in range(2)]
                V.tensor_tensor(fint[:, :, :], fraw[:, :, :], bc[1], ALU.mult).then_inc(fint_ready, 1)
                dve.wait_ge(fint_ready, m + 1)
                V.tensor_tensor(fraw[:, :, :], fint[:, :, :], bc[0], ALU.mult).then_inc(fw_ready, 1)

            group(0)
            with dve.Fori(1, LOOPED) as g:
                group(g)
            group(NG - 2)

            g = NG - 1
            seq, pos = units(g)[0], 0
            for c in range(NS):
                if c + 1 < NS:
                    maxima(g, c + 1)
                    inverse_sums(g, c + 1)
                if c == 0:
                    weight_scales(0)
                split(g, pos)
                pos += 1
                prob_low(g, c)
                if c:
                    out_low(g, c - 1)
                if pos in (3, 6):
                    weight_scales(pos // 3)
            out_low(g, NS - 1)
            while pos < len(seq):
                if seq[pos] == "W":
                    dve.wait_ge(pt_hi, g * (NS + 1) + NS + 1)
                    low(nullT[1][:, :], pt_bank[0:HEADS, 0:TG], nullT[0][:, :]).then_inc(pt_lo, 1)
                split(g, pos)
                pos += 1

            fc = [9]

            def link(ins):
                fc[0] += 1
                ins.then_inc(fchain, 1)
                dve.wait_ge(fchain, fc[0])

            def s1(i):
                return small[:, i:i + 1]

            def global_max(n):
                dve.wait_ge(gm_1, n + 1)
                V.reduce_max(small[0:1, 1:2], bank[0][0:1, 0:P], AX.X).then_inc(gm_t, 1)
                dve.wait_ge(gm_b, n + 1)

            dve.wait_ge(ln2_chain, ln2.per * NG)
            dve.wait_ge(x2_ready, NG)
            rsqrt(link, mean_var[:, :, 1], [rs3[:, i, :] for i in range(3)], EPS_LN)
            link(V.tensor_tensor(fa[:, 0, :], x2_max[:, :], mean_var[:, :, 0], ALU.subtract))
            link(V.tensor_tensor(fa[:, 1, :], mean_var[:, :, 0], x2_min[:, :], ALU.subtract))
            link(V.tensor_tensor(fa[:, 0, :], fa[:, 0, :], fa[:, 1, :], ALU.max))
            link(V.tensor_tensor(fa[:, 0, :], fa[:, 0, :], rs3[:, 0, :], ALU.mult))
            V.reduce_max(s1(0), fa[:, 0, :], AX.X).then_inc(gm_t, 1)
            global_max(0)
            link(V.tensor_scalar(s1(4), bank[1][:, 0:1], 1.0 / QMAX, MIN_SCALE, ALU.mult, ALU.max))
            link(V.reciprocal(s1(5), s1(4)))
            link(V.tensor_scalar(fa[:, 2, :], rs3[:, 0, :], s1(5), None, ALU.mult))
            link(V.scalar_tensor_tensor(out=fa[:, 3, :], in0=mean_var[:, :, 0], scalar=-1.0, in1=fa[:, 2, :],
                                        op0=ALU.mult, op1=ALU.mult))
            dve.wait_ge(x2all_in, 16)

            def x_low(t):
                dve.wait_ge(xt_hi, t + 1)
                low(xT[1][:, :, t * TG:(t + 1) * TG], unit_bank[t % 2][:, :].rearrange("p (k s) -> p k s", k=KD),
                    xT[0][:, :, t * TG:(t + 1) * TG]).then_inc(xt_lo, 1)

            for t in range(NT // 2):
                if t >= 2:
                    dve.wait_ge(xf_ready, t - 1)
                for b in range(2):
                    n = 2 * t + b
                    last = V.tensor_scalar(xi[:, t % 2, b, :], x2all[:, n, :], fa[:, 2, n:n + 1], fa[:, 3, n:n + 1],
                                           ALU.mult, ALU.add)
                last.then_inc(xi_ready, 1)
                if t >= 2:
                    x_low(t - 2)
            x_low(NT // 2 - 2)
            x_low(NT // 2 - 1)

            def gu_maximum(m, n):
                tg, j = n // KI, n % KI
                q = m * 4 * KI + n
                dve.wait_ge(gu_out, q + 1)
                last = V.tensor_reduce(amax[:, m, n:n + 1], (gate, up)[m][:, j, tg * 512:(tg + 1) * 512], AX.X,
                                       ALU.max, apply_absolute_value=True)
                return last

            def scale(n, src, factor, s, r, more=()):
                V.reduce_max(s1(0), src, AX.X).then_inc(gm_t, 1)
                global_max(n)
                link(V.tensor_scalar(s1(2), bank[1][:, 0:1], factor, None, ALU.mult))
                link(V.tensor_scalar(s1(s), s1(2), 1.0 / QMAX, MIN_SCALE, ALU.mult, ALU.max))
                link(V.reciprocal(s1(3), s1(s)))
                for dst, a, b in more:
                    link(V.tensor_scalar(s1(dst), a, b, None, ALU.mult))
                V.tensor_tensor(s1(r), s1(3), factor, ALU.mult).then_inc(scale_ready, 1)

            for n in range(4 * KI):
                last = gu_maximum(0, n)
            link(last)
            scale(1, amax[:, 0, :], s1(4), 10, 11, [(14, s1(10), 1.0 / 65536.0)])
            gate_c = gate[:, :, :].rearrange("p j t -> p (j t)")
            up_c = up[:, :, :].rearrange("p j t -> p (j t)")

            def gate_product(q):
                dve.wait_ge(sg_ready, q + 1)
                V.tensor_scalar(tsi[:, q % 2, :], tsg[:, q % 2, :], 65536.0, None, ALU.mult).then_inc(si_ready, 1)
                dve.wait_ge(si_ready, q + 1)
                link(V.tensor_tensor(gate_c[:, q * CH:(q + 1) * CH], tgi[:, q % 2, :], tsi[:, q % 2, :], ALU.mult))
                V.tensor_reduce(amax[:, 2, q:q + 1], gate_c[:, q * CH:(q + 1) * CH], AX.X, ALU.max,
                                apply_absolute_value=True).then_inc(p_ready, 1)

            for q in range(NCH):
                gu_maximum(1, 2 * q)
                gu_maximum(1, 2 * q + 1).then_inc(gu_max, 1)
                gate_product(q)
            dve.wait_ge(gu_max, NCH)
            dve.wait_ge(p_ready, NCH)
            scale(2, amax[:, 1, :], s1(4), 13, 12)
            scale(3, amax[:, 2, 0:NCH], s1(14), 15, 16, [(17, s1(15), s1(13))])
            for q in range(NCH):
                dve.wait_ge(pi_ready, q + 1)
                dve.wait_ge(ui_ready, q + 1)
                link(V.tensor_tensor(up_c[:, q * CH:(q + 1) * CH], tpi[:, q % 2, :], tui[:, q % 2, :], ALU.mult))
                V.tensor_reduce(amax[:, 3, q:q + 1], up_c[:, q * CH:(q + 1) * CH], AX.X, ALU.max,
                                apply_absolute_value=True).then_inc(o_ready, 1)
            dve.wait_ge(o_ready, NCH)
            scale(4, amax[:, 3, 0:NCH], s1(17), 18, 19, [(20, s1(18), gates[:, 1:2])])
            dve.wait_ge(scale_ready, 4)

            def finish(t):
                dve.wait_ge(down_done, 2 * t + 2)
                dve.wait_ge(xres_ld[t % 2], 16 * (t // 2 + 1))
                if t >= 2:
                    dve.wait_ge(y_out[t % 2], 16 * (t // 2))
                V.scalar_tensor_tensor(out=yout[:, t % 2, :, :],
                                       in0=bank[2 + t % 4][:, :].rearrange("p (b d) -> p b d", b=2),
                                       scalar=s1(20), in1=xres[:, t % 2, :, :], op0=ALU.mult,
                                       op1=ALU.add).then_inc(y_ready, 1)

            for n in range(4 * KI):
                tg, j = n // KI, n % KI
                if n >= 2:
                    dve.wait_ge(ol_ready, n - 1)
                V.tensor_scalar(tgi[:, n % 2, 0:512], up[:, j, tg * 512:(tg + 1) * 512], s1(19), None,
                                ALU.mult).then_inc(oi_ready, 1)
                dve.wait_ge(oh_ready, n + 1)
                low(oI[1][:, tg % 2, j, :], tgi[:, n % 2, 0:512], oI[0][:, tg % 2, j, :]).then_inc(ol_ready, 1)
                if tg >= 2 and j == 2:
                    finish(2 * tg - 4)
                if tg >= 2 and j == 4:
                    finish(2 * tg - 3)
            for t in range(4, 8):
                finish(t)

        @block.gpsimd
        def _(pool):
            G = nc.gpsimd
            row = lambda a: a.rearrange("(o n) -> o n", o=1)
            G.memset(ident[:, :], 0.0).then_inc(ident_zero, 1)
            pool.wait_ge(ident_zero, 1)
            G.affine_select(out=ident[:, :], in_=ident[:, :], compare_op=ALU.not_equal, fill=1.0, base=0,
                            pattern=[[-1, P]], channel_multiplier=1).then_inc(ident_ready, 1)
            pool.dma_start(gates[:, 0:1], row(g_xattn).to_broadcast([P, 1])).then_inc(const_in, 16)
            pool.dma_start(gates[:, 1:2], row(g_ffn).to_broadcast([P, 1])).then_inc(const_in, 16)
            pool.dma_start(gs[:, :], row(ln_scale).to_broadcast([P, D])).then_inc(const_in, 16)
            pool.dma_start(gb[:, :], row(ln_bias).to_broadcast([P, D])).then_inc(const_in, 16)
            with nc.allow_non_contiguous_dma(reason="one null key and value, 128 numbers"):
                for h in range(2):
                    pool.dma_start(ncol[h * DH:(h + 1) * DH, :], null_kv.rearrange("t d -> d t")).then_inc(const_in, 16)
            for i in range(2):
                last = G.memset(v[i][:, :, :, DH:2 * DH].bitcast(F32), 0.0)
            last.then_inc(vzero, 1)

            def normalise(g, c):
                pool.wait_ge(rinv_done, g * NS + c + 1)
                G.tensor_tensor(probs[:, c % 2, :, 0:S], probs[:, c % 2, :, 0:S],
                                rinv[:, c % 2, :].rearrange("p (u o) -> p u o", o=1).to_broadcast([P, 4, S]),
                                ALU.mult).then_inc(norm_done, 1)
                if c == 0 and not (isinstance(g, int) and g == 0):
                    wait(pool, pt_done, g * (NS + 1))
                G.tensor_tensor(pnull[:, :, 2 * c:2 * c + 2].rearrange("p b h -> p h b"),
                                probs[:, c % 2, :, S].rearrange("p (h b) -> p h b", h=2),
                                rinv[:, c % 2, :].rearrange("p (h b) -> p h b", h=2), ALU.mult).then_inc(pnull_done, 1)

            normalise(0, 0)
            pool.wait_ge(const_ready, 1)

            def group(g):
                for c in range(1, NS):
                    if c == 4:
                        pool.wait_ge(xres_in, 16 * (g + 1))
                        G.tensor_tensor(xr[:, :, :], xr[:, :, :],
                                        gb[:, :].rearrange("p (o d) -> p o d", o=1).to_broadcast([P, GB, D]),
                                        ALU.add).then_inc(xgb_ready, 1)
                    normalise(g, c)
                if not (isinstance(g, int) and g == NG - 1):
                    normalise(g + 1, 0)

            group(0)
            with pool.Fori(1, LOOPED) as g:
                group(g)
            group(NG - 2)

            g = NG - 1
            for c in range(1, NS):
                if c == 4:
                    pool.wait_ge(xres_in, 16 * (g + 1))
                    G.tensor_tensor(xr[:, :, :], xr[:, :, :],
                                    gb[:, :].rearrange("p (o d) -> p o d", o=1).to_broadcast([P, GB, D]),
                                    ALU.add).then_inc(xgb_ready, 1)
                normalise(g, c)

            gate_c = gate[:, :, :].rearrange("p j t -> p (j t)")
            pool.wait_ge(scale_ready, 1)
            for q in range(NCH):
                if q >= 2:
                    pool.wait_ge(p_ready, q - 1)
                G.tensor_scalar(tgi[:, q % 2, :], gate_c[:, q * CH:(q + 1) * CH], small[:, 11:12], 1.0,
                                ALU.mult, ALU.mult).then_inc(gi_ready, 1)
            pool.wait_ge(scale_ready, 3)
            for q in range(NCH):
                if q >= 2:
                    pool.wait_ge(o_ready, q - 1)
                G.tensor_scalar(tpi[:, q % 2, :], gate_c[:, q * CH:(q + 1) * CH], small[:, 16:17], 1.0,
                                ALU.mult, ALU.mult).then_inc(pi_ready, 1)


_INS = ['x', 'ctx_2048', 'g_xattn', 'g_ffn', 'L0_xattn_Wq', 'L0_xattn_Wkv', 'L0_xattn_null_kv', 'L0_xattn_Wout',
        'L0_xattn_ln_scale', 'L0_xattn_ln_bias', 'L0_ffn_w_gate', 'L0_ffn_w_up', 'L0_ffn_w_down']


def kernel(**inputs):
    import numpy as _np
    import concourse.bacc as _bacc
    from concourse import mybir as _mybir
    from concourse.bass_utils import run_bass_kernel_spmd as _run

    nc = _bacc.Bacc("TRN2", target_bir_lowering=False, num_devices=1)
    arrays, args = {}, []
    for name in _INS:
        a = _np.ascontiguousarray(inputs[name])
        arrays[f"in_{name}"] = a
        args.append(nc.dram_tensor(f"in_{name}", a.shape, _mybir.dt.from_np(a.dtype), kind="ExternalInput").ap())
    shape = arrays["in_x"].shape
    args.append(nc.dram_tensor("out_0", shape, _mybir.dt.float32, kind="ExternalOutput").ap())
    gated_cross_attention_ffn(nc, *args)
    return _run(nc, [arrays], core_ids=[0]).results[0]["out_0"]
```

```python
from contextlib import ExitStack

import concourse.bass as bass
from concourse import mybir

ALU = mybir.AluOpType
ACT = mybir.ActivationFunctionType
AX = mybir.AxisListType
F32 = mybir.dt.float32
F32R = mybir.dt.float32r
I16 = mybir.dt.int16
U16 = mybir.dt.uint16
I32 = mybir.dt.int32

P = 128
EPS_LN = 1e-5
EPS_OUT = 1e-6
QMAX = 32767.0
WMAX = 7.0
WBLOCK = 32
MIN_SCALE = 1e-12
RSQRT_MAGIC = 1597463007.0
NEWTON = 3

TERMS = ((0, 0), (0, 1), (1, 0))


def wait(engine, sem, value):
    if not isinstance(value, int) or value > 0:
        engine.wait_ge(sem, value)


class Chain:

    def __init__(self, engine, sem, per):
        self.engine, self.sem, self.per = engine, sem, per

    def start(self, call):
        self.base, self.k = call * self.per, 0

    def link(self, ins):
        self.k += 1
        ins.then_inc(self.sem, 1)
        self.engine.wait_ge(self.sem, self.base + self.k)

    def end(self):
        assert self.k == self.per, (self.k, self.per)


def gated_cross_attention_ffn(nc, x, ctx, g_xattn, g_ffn, Wq, Wkv, null_kv, Wout, ln_scale, ln_bias,
                              w_gate, w_up, w_down, out):
    B, S, D = x.shape
    C = ctx.shape[2]
    INNER = Wq.shape[1]
    DH = null_kv.shape[1]
    HEADS = INNER // DH
    I = w_gate.shape[0]
    GB = 2
    NG = B // GB
    TG = GB * S
    KD, KC, KF = D // P, C // P, INNER // P
    NS = KF
    KI = I // P
    NT = B * S // P
    QW = S + 2
    NK = S + 1
    NBK = I * D // P // WBLOCK
    SCALE = float(DH) ** -0.5

    PRO = ["X", "Ca", "Cb"] + [f"Q{c}" for c in range(NS)] + ["V00", "V10", "V01", "V11", "X", "Ca", "Cb", "W"]
    BODY = ["Q0", "Q1", "Q2", "Q3", "Q4", "Q5", "V00", "Q6", "V10", "Q7", "V01", "V11", "X", "Ca", "Cb", "W"]
    PENULT = [u for u in BODY if u not in ("X", "Ca", "Cb")]
    FINAL = [f"F{i}" for i in range(9)] + ["W"]
    LOOPED = NG - 2

    def units(g):
        if isinstance(g, str):
            return PRO, 0
        if isinstance(g, int) and g == NG - 1:
            return FINAL, len(PRO) + LOOPED * len(BODY) + len(PENULT)
        return (PENULT if isinstance(g, int) and g == LOOPED else BODY), g * len(BODY) + len(PRO)

    def is_split(kind):
        return kind[0] in "XCF"

    def copied(g, pos):
        first = units(g)[1]
        if isinstance(g, str):
            return pos + 1
        if isinstance(g, int) and g == NG - 1:
            return first - (NG - 1) + pos + 1
        return g * (len(BODY) - 1) + len(PRO) + pos + 1

    def low_made(g, pos):
        if isinstance(g, str):
            return sum(map(is_split, PRO[:pos + 1]))
        before = LOOPED if isinstance(g, int) and g > LOOPED else g
        return before * sum(map(is_split, BODY)) + sum(map(is_split, PRO)) + sum(map(is_split, units(g)[0][:pos + 1]))

    def parity(g, pos):
        if isinstance(g, str) or isinstance(g, int):
            return (units(g)[1] + pos) % 2
        return (len(PRO) + pos) % 2

    def feeds(g):
        return not isinstance(g, int) or g < LOOPED

    x_t = x.rearrange("b s d -> s b d")
    ctx_t = ctx.rearrange("b s d -> s b d")
    out_t = out.rearrange("b s d -> s b d")
    x2_dram = nc.dram_tensor("x2_scratch", (B, S, D), F32, kind="Internal").ap()
    x2_t = x2_dram.rearrange("b s d -> s b d")

    keep, att, ffn = ExitStack(), ExitStack(), ExitStack()
    with keep:
        stack = [keep]

        def sb(name, shape, dt=F32):
            return stack[0].enter_context(nc.sbuf_tensor(name, shape, dt))

        def sem(name):
            return keep.enter_context(nc.semaphore(name))

        ident = sb("ident", [P, P])
        ones = sb("ones", [1, P])
        gates = sb("gates", [P, 2])
        mean_var = sb("mean_var", [P, NT, 2])
        x2_max = sb("x2_max", [P, NT])
        x2_min = sb("x2_min", [P, NT])
        pause = sb("pause", [P, 1])
        small = sb("small", [P, 64])

        stack[0] = att
        wkv = [sb(f"wkv{i}", [P, KC, 2 * INNER], F32R) for i in range(2)]
        wq = [sb(f"wq{i}", [P, KD, INNER], F32R) for i in range(2)]
        wout = [sb(f"wout{i}", [P, KF, D], F32R) for i in range(2)]
        fraw = sb("fraw", [P, 3, NBK, WBLOCK])
        fint = sb("fint", [P, NBK, WBLOCK], I16)
        fs = sb("fs", [P, 2, NBK])
        qk = sb("qk", [P, NS, 2 * GB, QW])
        v = sb("v", [P, GB, NS, P])
        xnT = [sb(f"xnT{i}", [P, KD, TG], F32R) for i in range(2)]
        ctxT = [sb(f"ctxT{i}", [P, KC, TG], F32R) for i in range(2)]
        wnull = [sb(f"wnull{i}", [HEADS, D], F32R) for i in range(2)]
        nullT = [sb(f"nullT{i}", [HEADS, TG], F32R) for i in range(2)]
        gs = sb("gs", [P, D])
        gb = sb("gb", [P, D])
        nmax = sb("nmax", [P, 2, 4])
        rowsum = sb("rowsum", [P, 2, 4])
        rinv = sb("rinv", [P, 2, 4])
        pnull = sb("pnull", [P, GB, HEADS])
        bn = sb("bn", [P, 4, 6])
        mv = sb("mv", [P, 4, 2])
        rs = sb("rs", [P, 8, 2])
        xa = sb("xa", [P, GB, D])
        xr = sb("xr", [P, GB, D])
        y = sb("y", [P, GB, D])
        craw = sb("craw", [P, GB, C])
        late = ExitStack()
        stack[0] = late
        probs = sb("probs", [P, 2, 4, QW])
        pT = sb("pT", [P, 2, 4, P])
        oT = [sb(f"oT{i}", [P, KF, TG], F32R) for i in range(2)]
        late.close()
        stack[0] = late = ExitStack()
        NST = 7
        STW = 1024
        stage = sb("stage", [P, NST, STW])
        nkw = sb("nkw", [P, NS * GB, 2])
        nvm = sb("nvm", [P, KF, HEADS])
        nvr = [sb(f"nvr{i}", [P, KF, HEADS], F32R) for i in range(2)]
        ncol = sb("ncol", [P, 2])
        late.close()
        att.close()

        stack[0] = ffn
        wg = [sb(f"wg{i}", [P, KD, I], F32R) for i in range(2)]
        wu = [sb(f"wu{i}", [P, KD, I], F32R) for i in range(2)]
        wd = [sb(f"wd{i}", [P, KI, D], F32R) for i in range(2)]
        early = ExitStack()
        stack[0] = early
        x2all = sb("x2all", [P, NT, D])
        early.close()
        stack[0] = ffn
        up = sb("up", [P, KI, B * S])
        xT = [sb(f"xT{i}", [P, KD, B * S], F32R) for i in range(2)]
        early = ExitStack()
        stack[0] = early
        gate = sb("gate", [P, KI, B * S])
        early.close()
        early = ExitStack()
        stack[0] = early
        oI = [sb(f"oI{i}", [P, 2, KI, 512], F32R) for i in range(2)]
        early.close()
        early = ExitStack()
        stack[0] = ffn
        gate_pad = sb("gate_pad", [P, KI, B * S])
        CH = 1024
        NCH = KI * B * S // CH
        tgi = sb("tgi", [P, 2, CH], I16)
        tsg = sb("tsg", [P, 2, CH])
        tsi = sb("tsi", [P, 2, CH], U16)
        tpi = sb("tpi", [P, 2, CH], I16)
        tui = sb("tui", [P, 2, CH], I16)
        xi = sb("xi", [P, 2, 2, D], I16)
        xf = sb("xf", [P, 2, 2, D])
        xres = sb("xres", [P, 2, 2, D])
        yout = sb("yout", [P, 2, 2, D])
        fa = sb("fa", [P, 4, NT])
        rs3 = sb("rs3", [P, 4, NT])
        amax = sb("amax", [P, 4, 24])
        ffn.close()

        bank = [keep.enter_context(nc.psum_tensor(f"bank{i}", [P, 512], F32)) for i in range(8)]
        score_bank = [[bank[0], bank[1]], [bank[2], bank[3]]]
        pt_bank, pv_bank = bank[4], bank[5]
        unit_bank = [bank[6], bank[7]]

        stage_in = [sem(f"stage_in{i}") for i in range(NST)]
        wsplit_hi, wsplit_lo = sem("wsplit_hi"), sem("wsplit_lo")
        const_in, const_ready, null_ready = sem("const_in"), sem("const_ready"), sem("null_ready")
        ident_ready, ident_zero = sem("ident_ready"), sem("ident_zero")
        tanh_done = sem("tanh_done")
        x_in, ctx_in, xres_in, x2_out = sem("x_in"), sem("ctx_in"), sem("xres_in"), sem("x2_out")
        xn_ready = sem("xn_ready")
        unit_done, unit_hi, unit_lo, w_free = sem("unit_done"), sem("unit_hi"), sem("unit_lo"), sem("w_free")
        scores_done, max_done, exp_done = sem("scores_done"), sem("max_done"), sem("exp_done")
        rinv_done, norm_done, pnull_done = sem("rinv_done"), sem("norm_done"), sem("pnull_done")
        pt_done, pt_copied, null_hi = sem("pt_done"), sem("pt_copied"), sem("null_hi")
        pv_done, ot_hi, ot_lo = sem("pv_done"), sem("ot_hi"), sem("ot_lo")
        ln1_chain, ln2_chain, ln3_chain, prep_chain = (sem("ln1_chain"), sem("ln2_chain"), sem("ln3_chain"),
                                                       sem("prep_chain"))
        xgb_ready, ln_scaled, x2_ready, x2_stats = sem("xgb_ready"), sem("ln_scaled"), sem("x2_ready"), sem("x2_stats")
        fint_ready, fw_ready = sem("fint_ready"), sem("fw_ready")
        fraw_in = [sem(f"fraw_in{i}") for i in range(3)]
        x2all_in = sem("x2all_in")
        fchain, gm_t, gm_1, gm_b = sem("fchain"), sem("gm_t"), sem("gm_1"), sem("gm_b")
        scale_ready = sem("scale_ready")
        xi_ready, xf_ready, xt_done, xt_hi, xt_lo = (sem("xi_ready"), sem("xf_ready"), sem("xt_done"),
                                                     sem("xt_hi"), sem("xt_lo"))
        gu_done, gu_out, gu_max = sem("gu_done"), sem("gu_out"), sem("gu_max")
        gi_ready, sg_ready, si_ready, p_ready, pi_ready = (sem("gi_ready"), sem("sg_ready"), sem("si_ready"),
                                                           sem("p_ready"), sem("pi_ready"))
        ui_ready, o_ready, oi_ready, oh_ready, ol_ready = (sem("ui_ready"), sem("o_ready"), sem("oi_ready"),
                                                           sem("oh_ready"), sem("ol_ready"))
        down_done, y_ready = sem("down_done"), sem("y_ready")
        xres_ld = [sem(f"xres_ld{i}") for i in range(2)]
        y_out = [sem(f"y_out{i}") for i in range(2)]

        block = keep.enter_context(nc.Block())

        wq_r = Wq.rearrange("(k p) f -> p k f", p=P)
        wkv_r = Wkv.rearrange("(k p) f -> p k f", p=P)
        wout_r = Wout.rearrange("(k p) f -> p k f", p=P)
        pieces = [([w[:, k, :] for w in wq], wq_r[:, k, :], SCALE, None) for k in range(KD)]
        pieces += [([w[:, k, 0:INNER] for w in wkv], wkv_r[:, k, 0:INNER], 1.0, None) for k in range(KC)]
        pieces += [([w[:, k, INNER:] for w in wkv], wkv_r[:, k, INNER:], 1.0, None) for k in range(KC)]
        pieces += [([w[:, 4 * j:4 * j + 4, :] for w in wout], wout_r[:, 4 * j:4 * j + 4, :], 1.0, 4) for j in range(2)]
        NPC = len(pieces)
        READY_Q, READY_K, READY_V = KD, KD + KC, KD + 2 * KC

        def stage_view(i, fold):
            s = stage[:, i % NST, :]
            return s if fold is None else s.rearrange("p (a b) -> p a b", a=fold)

        fw_r = [w_gate.rearrange("(j p) h -> p j h", p=P), w_up.rearrange("(j p) h -> p j h", p=P), w_down.rearrange("(j p) i -> p j i", p=P)]

        def unit_view(kind, hl):
            if kind[0] == "Q":
                return qk[:, int(kind[1]), :, 0:S]
            if kind[0] == "V":
                b, h = int(kind[1]), int(kind[2])
                return v[:, b, 4 * h:4 * h + 4, :].rearrange("p c d -> p (c d)")
            if kind == "X":
                return xnT[hl][:, :, :]
            if kind[0] == "C":
                b = "ab".index(kind[1])
                return ctxT[hl][:, :, b * S:(b + 1) * S]
            i = int(kind[1])
            m, r = i // 3, i % 3
            if m < 2:
                return (wg, wu)[m][hl][:, :, 2 * r * P:(2 * r + 2) * P]
            return wd[hl][:, 2 * r:2 * r + 2, :]

        def unit_psum(kind, bk):
            if kind[0] == "Q":
                return bk[:, :].rearrange("p (a s) -> p a s", s=S)
            if kind[0] == "V":
                return bk[:, :]
            if kind[0] == "C":
                return bk[:, :].rearrange("p (a s) -> p a s", s=S)
            return bk[:, :].rearrange("p (a s) -> p a s", s=2 * P)

        @block.sync
        def _(sp):
            sp.dma_start(xa[:, :, :], x_t[:, 0:GB, :]).then_inc(x_in, 16)
            sp.dma_start(craw[:, :, :], ctx_t[:, 0:GB, :]).then_inc(ctx_in, 16)
            for i, (_, src, _, fold) in enumerate(pieces):
                if i >= NST:
                    sp.wait_ge(wsplit_lo, i - NST + 1)
                sp.dma_start(stage_view(i, fold), src).then_inc(stage_in[i % NST], 16)
                if i == 6:
                    sp.wait_ge(unit_done, 1)
                    sp.dma_start(xa[:, :, :], x_t[:, GB:2 * GB, :]).then_inc(x_in, 16)
                if i == 7:
                    sp.wait_ge(unit_done, 3)
                    sp.dma_start(craw[:, :, :], ctx_t[:, GB:2 * GB, :]).then_inc(ctx_in, 16)

            for m in range(3):
                sp.dma_start(fraw[:, m, :, :].rearrange("p n w -> p (n w)").rearrange(
                    "p (j h) -> p j h", j=(KI, KI, 2)[m]), fw_r[m]).then_inc(fraw_in[m], 16)

            def group_dma(g):
                if feeds(g):
                    sp.wait_ge(unit_done, g * len(BODY) + len(PRO) - 3)
                    sp.dma_start(xa[:, :, :], x_t[:, bass.ds((g + 2) * GB, GB), :]).then_inc(x_in, 16)
                    sp.wait_ge(unit_done, g * len(BODY) + len(PRO) - 1)
                    sp.dma_start(craw[:, :, :], ctx_t[:, bass.ds((g + 2) * GB, GB), :]).then_inc(ctx_in, 16)
                if not (isinstance(g, int) and g == 0):
                    sp.wait_ge(x2_ready, g)
                    sp.dma_start(x2_t[:, bass.ds((g - 1) * GB, GB), :], y[:, :, :]).then_inc(x2_out, 16)
                sp.dma_start(xr[:, :, :], x_t[:, bass.ds(g * GB, GB), :]).then_inc(xres_in, 16)

            group_dma(0)
            with sp.Fori(1, LOOPED) as g:
                group_dma(g)
            group_dma(NG - 2)
            group_dma(NG - 1)
            sp.wait_ge(unit_done, units(NG - 1)[1])
            sp.wait_ge(x2_out, 16 * (NG - 1))
            sp.dma_start(x2all[:, 0:(NG - 1) * GB, :], x2_t[:, 0:(NG - 1) * GB, :]).then_inc(x2all_in, 16)
            sp.wait_ge(x2_ready, NG)
            sp.dma_start(x2_t[:, (NG - 1) * GB:, :], x2all[:, (NG - 1) * GB:, :]).then_inc(x2_out, 16)
            sp.wait_ge(x2_out, 16 * NG)
            sp.wait_ge(xi_ready, NT // 2)

            def load_residual(t):
                sp.dma_start(xres[:, t % 2, :, :], x2_t[:, 2 * t:2 * t + 2, :]).then_inc(xres_ld[t % 2], 16)

            load_residual(0)
            load_residual(1)
            for t in range(NT // 2):
                sp.wait_ge(y_ready, t + 1)
                sp.dma_start(out_t[:, 2 * t:2 * t + 2, :], yout[:, t % 2, :, :]).then_inc(y_out[t % 2], 16)
                if t + 2 < NT // 2:
                    load_residual(t + 2)
            for i in range(2):
                sp.wait_ge(y_out[i], 16 * (NT // 4))

        @block.tensor
        def _(pe):
            mm = nc.tensor.matmul

            def unit_read(g, pos):
                if is_split(units(g)[0][pos]):
                    pe.wait_ge(unit_lo, low_made(g, pos))
                else:
                    pe.wait_ge(unit_hi, copied(g, pos))

            def unit(g, pos):
                seq = units(g)[0]
                kind, bk = seq[pos], unit_bank[parity(g, pos)]
                if pos >= 2:
                    unit_read(g, pos - 2)
                elif pos == 1 and not isinstance(g, str):
                    pe.wait_ge(w_free, g + 1)
                elif pos == 0 and isinstance(g, int) and g == NG - 1:
                    unit_read(g - 1, len(PENULT) - 2)
                elif not isinstance(g, str):
                    pe.wait_ge(unit_lo, low_made(g, -1))
                if kind[0] == "Q":
                    c = int(kind[1])
                    if isinstance(g, str) and c == 0:
                        pe.wait_ge(unit_lo, low_made(g, 2))
                        pe.wait_ge(wsplit_lo, READY_K)
                    elif c == 0:
                        pe.wait_ge(unit_lo, low_made(g, -1))
                    f = slice(c * P, (c + 1) * P)
                    for n, (wt, act_t, kk) in enumerate(((wq, xnT, KD), (wkv, ctxT, KC))):
                        for k in range(kk):
                            for i, (a, b) in enumerate(TERMS):
                                last = mm(bk[:, n * TG:(n + 1) * TG], wt[a][:, k, f], act_t[b][:, k, :],
                                          start=(k == 0 and i == 0), stop=(k == kk - 1 and i == len(TERMS) - 1))
                elif kind[0] == "V":
                    b, h = int(kind[1]), int(kind[2])
                    if isinstance(g, str) and pos == PRO.index("V00"):
                        pe.wait_ge(wsplit_lo, READY_V)
                    for k in range(KC):
                        for i, (a, w) in enumerate(TERMS):
                            last = mm(bk[:, :], ctxT[a][:, k, b * S:(b + 1) * S],
                                      wkv[w][:, k, INNER + h * 512:INNER + (h + 1) * 512],
                                      start=(k == 0 and i == 0), stop=(k == KC - 1 and i == len(TERMS) - 1))
                elif kind == "X":
                    n = (0 if pos == 0 else 1) if isinstance(g, str) else g + 2
                    if isinstance(g, str) and pos == 0:
                        pe.wait_ge(ident_ready, 1)
                    pe.wait_ge(xn_ready, n + 1)
                    for k in range(KD):
                        for b in range(GB):
                            last = nc.tensor.transpose(bk[:, k * TG + b * S:k * TG + (b + 1) * S],
                                                       xa[:, b, k * P:(k + 1) * P], ident[:, :])
                elif kind[0] == "C":
                    b = "ab".index(kind[1])
                    n = (0 if pos < 3 else 1) if isinstance(g, str) else g + 2
                    if b == 0:
                        pe.wait_ge(ctx_in, (n + 1) * 16)
                    for k in range(KC):
                        last = nc.tensor.transpose(bk[:, k * S:(k + 1) * S], craw[:, b, k * P:(k + 1) * P],
                                                   ident[:, :])
                elif kind[0] == "F":
                    i = int(kind[1])
                    m, r = i // 3, i % 3
                    if r == 0:
                        pe.wait_ge(fw_ready, m + 1)
                    wf = fraw[:, m, :, :].rearrange("p n w -> p (n w)")
                    for a in range(2):
                        for b in range(2):
                            src = ((2 * r + b) * D + a * P) if m < 2 else (b * I + (2 * r + a) * P)
                            last = nc.tensor.transpose(bk[:, (2 * a + b) * P:(2 * a + b + 1) * P],
                                                       wf[:, src:src + P], ident[:, :])
                elif isinstance(g, str):
                    pe.wait_ge(null_ready, 2)
                    pe.wait_ge(wsplit_lo, NPC)
                    for k in range(KF):
                        for i, (a, w) in enumerate(TERMS):
                            last = mm(bk[0:HEADS, 0:D], nvr[a][:, k, :], wout[w][:, k, :],
                                      start=(k == 0 and i == 0), stop=(k == KF - 1 and i == len(TERMS) - 1))
                else:
                    wait(pe, ot_lo, g * NS + NS)
                    wait(pe, pt_copied, g * (NS + 1) + NS + 1)
                    pe.wait_ge(w_free, g + 1)
                    for b in range(GB):
                        o = bk[:, b * D:(b + 1) * D]
                        for k in range(KF):
                            for i, (a, w) in enumerate(TERMS):
                                mm(o, oT[a][:, k, b * S:(b + 1) * S], wout[w][:, k, :],
                                   start=(k == 0 and i == 0), stop=False)
                        for i, (a, w) in enumerate(TERMS):
                            last = mm(o, nullT[a][:, b * S:(b + 1) * S], wnull[w][:, :],
                                      start=False, stop=(i == len(TERMS) - 1))
                last.then_inc(unit_done, 1)

            def scores(g, c):
                wait(pe, exp_done, g * NS + c - 1)
                for b in range(GB):
                    for h in range(2):
                        rows = slice(h * DH, (h + 1) * DH)
                        last = mm(score_bank[c % 2][h][:, b * QW:b * QW + QW], qk[rows, c, b, 0:S],
                                  qk[rows, c, GB + b, 0:QW], start=True, stop=True)
                last.then_inc(scores_done, 1)

            def prob_transposes(g, c):
                pe.wait_ge(norm_done, g * NS + c + 1)
                wait(pe, pt_copied, g * (NS + 1) + c)
                for u in range(4):
                    last = nc.tensor.transpose(pt_bank[:, u * P:(u + 1) * P], probs[:, c % 2, u, 0:S], ident[:, :])
                last.then_inc(pt_done, 1)

            def null_transposes(g):
                wait(pe, pnull_done, g * NS + NS)
                wait(pe, pt_copied, g * (NS + 1) + NS)
                for b in range(GB):
                    last = nc.tensor.transpose(pt_bank[0:HEADS, b * S:(b + 1) * S], pnull[:, b, :], ident[:, :])
                last.then_inc(pt_done, 1)

            def values(g, c):
                wait(pe, pt_copied, g * (NS + 1) + c + 1)
                wait(pe, ot_lo, g * NS + c)
                for b in range(GB):
                    for h in range(2):
                        rows = slice(h * DH, (h + 1) * DH)
                        last = mm(pv_bank[rows, b * S:(b + 1) * S], v[:, b, c, rows],
                                  pT[:, c % 2, 2 * h + b, :], start=True, stop=True)
                last.then_inc(pv_done, 1)

            for pos in range(len(PRO)):
                unit("pro", pos)
                if PRO[pos] == "Q7":
                    pe.wait_ge(null_ready, 1)
                    scores(0, 0)

            def group(g):
                final = isinstance(g, int) and g == NG - 1
                pos = 0
                seq = units(g)[0]
                for c in range(NS):
                    if c + 1 < NS:
                        scores(g, c + 1)
                    todo = [seq[pos]] if final else [s for s in (f"Q{c}", {5: "V00", 6: "V10"}.get(c)) if s]
                    for s in todo:
                        assert seq[pos] == s
                        unit(g, pos)
                        pos += 1
                    prob_transposes(g, c)
                    if c:
                        values(g, c - 1)
                if not final:
                    scores(g + 1, 0)
                values(g, NS - 1)
                while pos < len(seq):
                    if seq[pos] in ("X", "W") and (seq[pos] == "X" or "X" not in seq):
                        null_transposes(g)
                    unit(g, pos)
                    pos += 1

            group(0)
            with pe.Fori(1, LOOPED) as g:
                group(g)
            group(NG - 2)
            group(NG - 1)

            def global_max(n):
                pe.wait_ge(gm_t, 2 * n + 1)
                nc.tensor.transpose(bank[0][0:1, 0:P], small[:, 0:1], ident[:, :]).then_inc(gm_1, 1)
                pe.wait_ge(gm_t, 2 * n + 2)
                mm(bank[1][:, 0:1], ones[:, :], small[0:1, 1:2], start=True, stop=True).then_inc(gm_b, 1)

            global_max(0)
            for t in range(NT // 2):
                pe.wait_ge(xf_ready, t + 1)
                if t >= 2:
                    pe.wait_ge(xt_lo, t - 1)
                for k in range(KD):
                    for b in range(2):
                        last = nc.tensor.transpose(unit_bank[t % 2][:, (2 * k + b) * P:(2 * k + b + 1) * P],
                                                   xf[:, t % 2, b, k * P:(k + 1) * P], ident[:, :])
                last.then_inc(xt_done, 1)

            for m in range(2):
                for tg in range(4):
                    for j in range(KI):
                        n = (m * 4 + tg) * KI + j
                        if m == 0 and j == 0:
                            pe.wait_ge(xt_lo, 2 * tg + 2)
                        bk = bank[2 + n % 4]
                        if n >= 4:
                            pe.wait_ge(gu_out, n - 3)
                        for k in range(KD):
                            for i, (a, w) in enumerate(TERMS):
                                last = mm(bk[:, :], (wg, wu)[m][a][:, k, j * P:(j + 1) * P],
                                          xT[w][:, k, tg * 512:(tg + 1) * 512],
                                          start=(k == 0 and i == 0), stop=(k == KD - 1 and i == len(TERMS) - 1))
                        last.then_inc(gu_done, 1)
                        if m == 1 and tg == 0 and j == 3:
                            global_max(1)
            for n in range(2, 5):
                global_max(n)
            for t in range(NT):
                tg = t // 4
                if t % 4 == 0:
                    pe.wait_ge(ol_ready, (tg + 1) * KI)
                bk = bank[2 + (t // 2) % 4]
                if t % 2 == 0 and t >= 8:
                    pe.wait_ge(y_ready, t // 2 - 3)
                for j in range(KI):
                    for i, (a, w) in enumerate(TERMS):
                        last = mm(bk[:, (t % 2) * D:(t % 2 + 1) * D], oI[a][:, tg % 2, j, (t % 4) * P:(t % 4 + 1) * P],
                                  wd[w][:, j, :], start=(j == 0 and i == 0), stop=(j == KI - 1 and i == 2))
                last.then_inc(down_done, 1)

        @block.scalar
        def _(act):
            act_copy = ACT.Copy

            def high(dst, src, scale=1.0):
                return nc.scalar.activation(dst, src, act_copy, scale=scale)

            act.wait_ge(const_in, 16 * 6)
            nc.scalar.activation(gates[:, :], gates[:, :], ACT.Tanh).then_inc(tanh_done, 1)

            def split(g, pos):
                seq, first = units(g)
                kind = seq[pos]
                if kind == "W" and not isinstance(g, str):
                    return
                act.wait_ge(unit_done, first + pos + 1)
                if kind == "W":
                    high(wnull[0][:, :], unit_bank[parity(g, pos)][0:HEADS, 0:D]).then_inc(unit_hi, 1)
                else:
                    high(unit_view(kind, 0), unit_psum(kind, unit_bank[parity(g, pos)])).then_inc(unit_hi, 1)

            def exps(g, c):
                act.wait_ge(max_done, g * NS + c + 1)
                if not (isinstance(g, int) and g == 0 and c < 2):
                    if c == 0:
                        wait(act, pt_done, g * (NS + 1) - 2)
                    else:
                        wait(act, pt_done, g * (NS + 1) + (c - 1 if c > 1 else 0))
                    wait(act, pnull_done, g * NS + c - 1)
                for u in range(4):
                    h, b = u // 2, u % 2
                    last = nc.scalar.activation(probs[:, c % 2, u, 0:NK],
                                                score_bank[c % 2][h][:, b * QW:b * QW + NK], ACT.Exp,
                                                bias=nmax[:, c % 2, u:u + 1], accum_out=rowsum[:, c % 2, u:u + 1])
                last.then_inc(exp_done, 1)

            def out_high(g, c):
                wait(act, pv_done, g * NS + c + 1)
                high(oT[0][:, c, :], pv_bank[:, 0:TG]).then_inc(ot_hi, 1)

            npos = [0]
            for i, (dst, _, f, fold) in enumerate(pieces):
                if i in (READY_Q, READY_K - 1):
                    for _ in range(2 if i == READY_Q else 1):
                        split("pro", npos[0])
                        npos[0] += 1
                act.wait_ge(stage_in[i % NST], 16 * (i // NST + 1))
                high(dst[0], stage_view(i, fold), f).then_inc(wsplit_hi, 1)
                if i >= READY_K and PRO[npos[0]] != "V00":
                    split("pro", npos[0])
                    npos[0] += 1
            while npos[0] < len(PRO):
                split("pro", npos[0])
                if PRO[npos[0]] == "Q7":
                    exps(0, 0)
                npos[0] += 1

            def group(g):
                final = isinstance(g, int) and g == NG - 1
                seq, pos = units(g)[0], 0
                for c in range(NS):
                    if c + 1 < NS:
                        exps(g, c + 1)
                    for s in ([0] if final else [s for s in (f"Q{c}", {5: "V00", 6: "V10"}.get(c)) if s]):
                        split(g, pos)
                        pos += 1
                    if c:
                        out_high(g, c - 1)
                if not final:
                    exps(g + 1, 0)
                out_high(g, NS - 1)
                while pos < len(seq):
                    if seq[pos] in ("X", "W") and (seq[pos] == "X" or "X" not in seq):
                        wait(act, pt_done, g * (NS + 1) + NS + 1)
                        high(nullT[0][:, :], pt_bank[0:HEADS, 0:TG]).then_inc(null_hi, 1)
                    split(g, pos)
                    pos += 1

            group(0)
            with act.Fori(1, LOOPED) as g:
                group(g)
            group(NG - 2)
            group(NG - 1)

            for t in range(NT // 2):
                act.wait_ge(xi_ready, t + 1)
                if t >= 2:
                    act.wait_ge(xt_done, t - 1)
                high(xf[:, t % 2, :, :], xi[:, t % 2, :, :]).then_inc(xf_ready, 1)
                if t >= 1:
                    act.wait_ge(xt_done, t)
                    high(xT[0][:, :, (t - 1) * TG:t * TG],
                         unit_bank[(t - 1) % 2][:, :].rearrange("p (k s) -> p k s", k=KD)).then_inc(xt_hi, 1)
            t = NT // 2
            act.wait_ge(xt_done, t)
            high(xT[0][:, :, (t - 1) * TG:t * TG],
                 unit_bank[(t - 1) % 2][:, :].rearrange("p (k s) -> p k s", k=KD)).then_inc(xt_hi, 1)

            def gu(m, n):
                tg, j = n // KI, n % KI
                q = m * 4 * KI + n
                act.wait_ge(gu_done, q + 1)
                nc.scalar.activation((gate, up)[m][:, j, tg * 512:(tg + 1) * 512], bank[2 + q % 4][:, :],
                                     act_copy).then_inc(gu_out, 1)

            for n in range(4 * KI):
                gu(0, n)
            gate_c = gate[:, :, :].rearrange("p j t -> p (j t)")
            up_c = up[:, :, :].rearrange("p j t -> p (j t)")
            act.wait_ge(x2_out, 16 * NG)
            for q in range(NCH):
                gu(1, 2 * q)
                gu(1, 2 * q + 1)
                act.wait_ge(gi_ready, q + 1)
                if q >= 2:
                    act.wait_ge(si_ready, q - 1)
                nc.scalar.activation(tsg[:, q % 2, :], tgi[:, q % 2, :], ACT.Sigmoid,
                                     scale=small[:, 10:11]).then_inc(sg_ready, 1)
            for q in range(NCH):
                if q == 0:
                    act.wait_ge(scale_ready, 2)
                if q >= 2:
                    act.wait_ge(o_ready, q - 1)
                nc.scalar.activation(tui[:, q % 2, :], up_c[:, q * CH:(q + 1) * CH], act_copy,
                                     scale=small[:, 12:13]).then_inc(ui_ready, 1)
            for n in range(4 * KI):
                act.wait_ge(oi_ready, n + 1)
                tg, j = n // KI, n % KI
                if tg >= 2 and j == 0:
                    act.wait_ge(down_done, 4 * (tg - 1))
                high(oI[0][:, tg % 2, j, :], tgi[:, n % 2, 0:512]).then_inc(oh_ready, 1)

        @block.vector
        def _(dve):
            V = nc.vector

            def low(dst, src, hi, f=1.0):
                if f == 1.0:
                    return V.tensor_tensor(dst, src, hi.bitcast(F32), ALU.subtract)
                return V.scalar_tensor_tensor(out=dst, in0=src, scalar=f, in1=hi.bitcast(F32), op0=ALU.mult,
                                              op1=ALU.subtract)

            def rsqrt(link, var, r, eps):
                link(V.tensor_scalar(r[1], var, eps, None, ALU.add))
                link(V.tensor_scalar(r[0].bitcast(I32), r[1].bitcast(I32), -0.5, RSQRT_MAGIC, ALU.mult, ALU.add))
                for _ in range(NEWTON):
                    link(V.scalar_tensor_tensor(out=r[2], in0=r[0], scalar=-0.5, in1=r[0],
                                                      op0=ALU.mult, op1=ALU.mult))
                    link(V.tensor_tensor(r[2], r[2], r[1], ALU.mult))
                    link(V.scalar_tensor_tensor(out=r[0], in0=r[2], scalar=1.5, in1=r[0],
                                                      op0=ALU.add, op1=ALU.mult))

            def settle():
                V.memset(pause[:, :], 0.0)

            NRS = 2 + 3 * NEWTON
            ln1 = Chain(dve, ln1_chain, 2 + NRS)
            ln2 = Chain(dve, ln2_chain, 2 + NRS)
            ln3 = Chain(dve, ln3_chain, 2)

            def ln_stats(n):
                dve.wait_ge(x_in, (n + 1) * 16)
                ln1.start(n)
                for b in range(GB):
                    last = V.bn_stats(bn[:, b, :], xa[:, b, :])
                ln1.link(last)
                settle()
                for b in range(GB):
                    last = V.bn_aggr(mv[:, b, :], bn[:, b, :])
                ln1.link(last)

            def ln_rstd():
                rsqrt(ln1.link, mv[:, 0:2, 1], [rs[:, i, :] for i in range(3)], EPS_LN)
                ln1.end()

            def ln_apply():
                for b in range(GB):
                    last = V.tensor_scalar(xa[:, b, :], xa[:, b, :], mv[:, b, 0:1], rs[:, 0, b:b + 1],
                                           ALU.subtract, ALU.mult)
                last.then_inc(xn_ready, 1)

            def split(g, pos):
                kind = units(g)[0][pos]
                bk = unit_bank[parity(g, pos)]
                if kind == "W" and isinstance(g, str):
                    dve.wait_ge(unit_hi, copied(g, pos))
                    low(wnull[1][:, :], bk[0:HEADS, 0:D], wnull[0][:, :]).then_inc(w_free, 1)
                elif is_split(kind):
                    dve.wait_ge(unit_hi, copied(g, pos))
                    low(unit_view(kind, 1), unit_psum(kind, bk), unit_view(kind, 0)).then_inc(unit_lo, 1)

            def attention_out(g):
                lastg = isinstance(g, int) and g == NG - 1
                seq, first = units(g)
                pos = seq.index("W")
                bk = unit_bank[parity(g, pos)]
                dve.wait_ge(unit_done, first + pos + 1)
                ln2.start(g)
                for b in range(GB):
                    last = V.bn_stats(bn[:, 2 + b, :], bk[:, b * D:(b + 1) * D])
                ln2.link(last)
                settle()
                for b in range(GB):
                    last = V.bn_aggr(mv[:, 2 + b, :], bn[:, 2 + b, :])
                ln2.link(last)
                if not lastg:
                    maxima(g + 1, 1)
                rsqrt(ln2.link, mv[:, 2:4, 1], [rs[:, 4 + i, :] for i in range(3)], EPS_OUT)
                ln2.end()
                dst = x2all[:, g * GB:(g + 1) * GB, :] if lastg else y[:, :, :]
                if not lastg:
                    wait(dve, x2_out, g * 16)
                for b in range(GB):
                    last = V.tensor_scalar(dst[:, b, :], bk[:, b * D:(b + 1) * D], mv[:, 2 + b, 0:1],
                                           rs[:, 4, b:b + 1], ALU.subtract, ALU.mult)
                last.then_inc(w_free, 1)

            def x2_statistics(g, src):
                ln3.start(g)
                for b in range(GB):
                    last = V.bn_stats(bn[:, 2 + b, :], src[:, b, :])
                ln3.link(last)
                settle()
                for b in range(GB):
                    last = V.bn_aggr(mv[:, 2 + b, :], bn[:, 2 + b, :])
                ln3.link(last)
                settle()
                V.tensor_copy(mean_var[:, bass.ds(g * GB, GB), :], mv[:, 2:4, :]).then_inc(x2_stats, 1)

            def x2_range(g, src):
                V.tensor_reduce(x2_max[:, bass.ds(g * GB, GB)], src, AX.X, ALU.max)
                V.tensor_reduce(x2_min[:, bass.ds(g * GB, GB)], src, AX.X, ALU.min).then_inc(x2_stats, 1)

            def maxima(g, c):
                dve.wait_ge(scores_done, g * NS + c + 1)
                for h in range(2):
                    last = V.tensor_reduce(nmax[:, c % 2, 2 * h:2 * h + 2],
                                           score_bank[c % 2][h][:, 0:GB * QW].rearrange(
                                               "p (b s) -> p b s", b=GB)[:, :, 0:NK],
                                           AX.X, ALU.max, negate=True)
                last.then_inc(max_done, 1)

            def inverse_sums(g, c):
                wait(dve, exp_done, g * NS + c + 1)
                V.reciprocal(rinv[:, c % 2, :], rowsum[:, c % 2, :]).then_inc(rinv_done, 1)

            def prob_copy(g, c):
                dve.wait_ge(pt_done, g * (NS + 1) + c + 1)
                V.tensor_copy(pT[:, c % 2, :, :], pt_bank[:, :].rearrange("p (u s) -> p u s", u=4)).then_inc(pt_copied, 1)

            def null_low(g):
                dve.wait_ge(null_hi, g + 1)
                low(nullT[1][:, :], pt_bank[0:HEADS, 0:TG], nullT[0][:, :]).then_inc(pt_copied, 1)

            def out_low(g, c):
                dve.wait_ge(ot_hi, g * NS + c + 1)
                low(oT[1][:, c, :], pv_bank[:, 0:TG], oT[0][:, c, :]).then_inc(ot_lo, 1)

            V.memset(ones[:, :], 1.0)
            V.memset(nkw[:, :, :], 0.0).then_inc(prep_chain, 1)
            V.memset(nvm[:, :, :], 0.0).then_inc(prep_chain, 1)
            ln_stats(0)
            ln_rstd()
            ln_apply()
            npos = [0]

            def constants():
                dve.wait_ge(tanh_done, 1)
                dve.wait_ge(prep_chain, 2)
                V.tensor_scalar(gs[:, :], gs[:, :], gates[:, 0:1], None, ALU.mult)
                V.tensor_scalar(gb[:, :], gb[:, :], gates[:, 0:1], None, ALU.mult).then_inc(const_ready, 1)
                V.tensor_scalar(nkw[:, :, 0:1], nkw[:, :, 0:1], ncol[:, 0:1], None, ALU.add)
                diag = nvm[:, :, :].rearrange("p k h -> p (k h)")
                for h in range(2):
                    rows = slice(h * DH, (h + 1) * DH)
                    d = diag[rows, h:h + (HEADS + 2) * (KF - 1) + 1:HEADS + 2]
                    last = V.tensor_scalar(d, d, ncol[rows, 1:2], None, ALU.add)
                last.then_inc(prep_chain, 1)
                dve.wait_ge(prep_chain, 3)
                V.tensor_copy(qk[:, :, GB:2 * GB, S:QW],
                              nkw[:, :, :].rearrange("p (c b) t -> p c b t", b=GB)).then_inc(null_ready, 1)
                V.tensor_copy(nvr[0][:, :, :], nvm[:, :, :]).then_inc(prep_chain, 1)
                dve.wait_ge(prep_chain, 4)
                low(nvr[1][:, :, :], nvm[:, :, :], nvr[0][:, :, :]).then_inc(null_ready, 1)

            for i, (dst, _, f, fold) in enumerate(pieces):
                if i in (READY_Q, READY_K - 1):
                    for _ in range(2 if i == READY_Q else 1):
                        split("pro", npos[0])
                        npos[0] += 1
                if i == READY_K - 1:
                    constants()
                dve.wait_ge(wsplit_hi, i + 1)
                low(dst[1], stage_view(i, fold), dst[0], f).then_inc(wsplit_lo, 1)
                if i >= READY_K and PRO[npos[0]] != "V00":
                    split("pro", npos[0])
                    npos[0] += 1
            while npos[0] < len(PRO):
                if PRO[npos[0]] == "V00":
                    ln_stats(1)
                    ln_rstd()
                    ln_apply()
                split("pro", npos[0])
                if PRO[npos[0]] == "Q7":
                    maxima(0, 0)
                    inverse_sums(0, 0)
                npos[0] += 1

            maxima(0, 1)

            def weight_scales(m):
                dve.wait_ge(fraw_in[m], 16)
                wait(dve, fw_ready, m)
                w = fraw[:, m, :, :]
                V.tensor_reduce(fs[:, 0, :], w, AX.X, ALU.max, apply_absolute_value=True).then_inc(fchain, 1)
                dve.wait_ge(fchain, 3 * m + 1)
                V.tensor_scalar(fs[:, 0, :], fs[:, 0, :], 1.0 / WMAX, MIN_SCALE, ALU.mult, ALU.max).then_inc(fchain, 1)
                dve.wait_ge(fchain, 3 * m + 2)
                V.reciprocal(fs[:, 1, :], fs[:, 0, :]).then_inc(fchain, 1)
                dve.wait_ge(fchain, 3 * m + 3)

            def weight_integers(m):
                bc = fs[:, 1, :].rearrange("p (n o) -> p n o", o=1).to_broadcast([P, NBK, WBLOCK])
                V.tensor_tensor(fint[:, :, :], fraw[:, m, :, :], bc, ALU.mult).then_inc(fint_ready, 1)

            def weight_values(m):
                bc = fs[:, 0, :].rearrange("p (n o) -> p n o", o=1).to_broadcast([P, NBK, WBLOCK])
                dve.wait_ge(fint_ready, m + 1)
                V.tensor_tensor(fraw[:, m, :, :], fint[:, :, :], bc, ALU.mult).then_inc(fw_ready, 1)

            def group(g):
                peeled, final = isinstance(g, int), isinstance(g, int) and g == NG - 1
                seq, pos = units(g)[0], 0
                for c in range(NS):
                    if 1 <= c < NS - 1:
                        maxima(g, c + 1)
                    if c < NS - 1:
                        inverse_sums(g, c + 1)
                    if final:
                        split(g, pos)
                        pos += 1
                    prob_copy(g, c)
                    if c:
                        out_low(g, c - 1)
                    if c == 3 and not (peeled and g == 0):
                        dve.wait_ge(x2_ready, g)
                        settle()
                        x2_statistics(g - 1, y[:, :, :])
                    if c == 4 and not (peeled and g == 0):
                        x2_range(g - 1, y[:, :, :])
                    if feeds(g) and c == 5:
                        ln_stats(g + 2)
                    if feeds(g) and c == 6:
                        ln_rstd()
                    if feeds(g) and c == 7:
                        ln_apply()
                    if peeled and g == NG - 2:
                        if c in (0, 2, 4):
                            weight_scales(c // 2)
                            weight_integers(c // 2)
                        elif c in (1, 3, 5):
                            weight_values(c // 2)
                if not final:
                    maxima(g + 1, 0)
                    inverse_sums(g + 1, 0)
                out_low(g, NS - 1)
                for n in range(pos if final else NS + 2, len(seq)):
                    if seq[n] == "X" or (seq[n] == "W" and "X" not in seq):
                        null_low(g)
                    split(g, n)
                attention_out(g)

            group(0)
            with dve.Fori(1, LOOPED) as g:
                group(g)
            group(NG - 2)
            group(NG - 1)

            g = NG - 1
            last2 = x2all[:, g * GB:(g + 1) * GB, :]
            dve.wait_ge(w_free, NG + 1)
            for b in range(GB):
                last = V.tensor_tensor(last2[:, b, :], last2[:, b, :], gs[:, :], ALU.mult)
            last.then_inc(ln_scaled, 1)
            dve.wait_ge(ln_scaled, NG)
            dve.wait_ge(xgb_ready, NG)
            V.tensor_tensor(last2, last2, xr[:, :, :], ALU.add).then_inc(x2_ready, 1)
            dve.wait_ge(x2_ready, NG)
            x2_statistics(g, last2)
            x2_range(g, last2)

            fc = [9]

            def link(ins):
                fc[0] += 1
                ins.then_inc(fchain, 1)
                dve.wait_ge(fchain, fc[0])

            def s1(i):
                return small[:, i:i + 1]

            def global_max(n):
                dve.wait_ge(gm_1, n + 1)
                V.reduce_max(small[0:1, 1:2], bank[0][0:1, 0:P], AX.X).then_inc(gm_t, 1)
                dve.wait_ge(gm_b, n + 1)

            dve.wait_ge(x2_stats, 2 * NG)
            rsqrt(link, mean_var[:, :, 1], [rs3[:, i, :] for i in range(3)], EPS_LN)
            link(V.tensor_tensor(fa[:, 0, :], x2_max[:, :], mean_var[:, :, 0], ALU.subtract))
            link(V.tensor_tensor(fa[:, 1, :], mean_var[:, :, 0], x2_min[:, :], ALU.subtract))
            link(V.tensor_tensor(fa[:, 0, :], fa[:, 0, :], fa[:, 1, :], ALU.max))
            link(V.tensor_tensor(fa[:, 0, :], fa[:, 0, :], rs3[:, 0, :], ALU.mult))
            V.reduce_max(s1(0), fa[:, 0, :], AX.X).then_inc(gm_t, 1)
            global_max(0)
            link(V.tensor_scalar(s1(4), bank[1][:, 0:1], 1.0 / QMAX, MIN_SCALE, ALU.mult, ALU.max))
            link(V.reciprocal(s1(5), s1(4)))
            link(V.tensor_scalar(fa[:, 2, :], rs3[:, 0, :], s1(5), None, ALU.mult))
            link(V.scalar_tensor_tensor(out=fa[:, 3, :], in0=mean_var[:, :, 0], scalar=-1.0, in1=fa[:, 2, :],
                                        op0=ALU.mult, op1=ALU.mult))
            dve.wait_ge(x2all_in, 16)

            def x_low(t):
                dve.wait_ge(xt_hi, t + 1)
                low(xT[1][:, :, t * TG:(t + 1) * TG], unit_bank[t % 2][:, :].rearrange("p (k s) -> p k s", k=KD),
                    xT[0][:, :, t * TG:(t + 1) * TG]).then_inc(xt_lo, 1)

            for t in range(NT // 2):
                if t >= 2:
                    dve.wait_ge(xf_ready, t - 1)
                for b in range(2):
                    n = 2 * t + b
                    last = V.tensor_scalar(xi[:, t % 2, b, :], x2all[:, n, :], fa[:, 2, n:n + 1], fa[:, 3, n:n + 1],
                                           ALU.mult, ALU.add)
                last.then_inc(xi_ready, 1)
                if t >= 2:
                    x_low(t - 2)
            x_low(NT // 2 - 2)
            x_low(NT // 2 - 1)

            def gu_maximum(m, n):
                tg, j = n // KI, n % KI
                q = m * 4 * KI + n
                dve.wait_ge(gu_out, q + 1)
                last = V.tensor_reduce(amax[:, m, n:n + 1], (gate, up)[m][:, j, tg * 512:(tg + 1) * 512], AX.X,
                                       ALU.max, apply_absolute_value=True)
                return last

            def scale(n, src, factor, s, r, more=()):
                V.reduce_max(s1(0), src, AX.X).then_inc(gm_t, 1)
                global_max(n)
                link(V.tensor_scalar(s1(2), bank[1][:, 0:1], factor, None, ALU.mult))
                link(V.tensor_scalar(s1(s), s1(2), 1.0 / QMAX, MIN_SCALE, ALU.mult, ALU.max))
                link(V.reciprocal(s1(3), s1(s)))
                for dst, a, b in more:
                    link(V.tensor_scalar(s1(dst), a, b, None, ALU.mult))
                V.tensor_tensor(s1(r), s1(3), factor, ALU.mult).then_inc(scale_ready, 1)

            for n in range(4 * KI):
                last = gu_maximum(0, n)
            link(last)
            scale(1, amax[:, 0, :], s1(4), 10, 11, [(14, s1(10), 1.0 / 65536.0)])
            gate_c = gate[:, :, :].rearrange("p j t -> p (j t)")
            up_c = up[:, :, :].rearrange("p j t -> p (j t)")

            def gate_product(q):
                dve.wait_ge(sg_ready, q + 1)
                V.tensor_scalar(tsi[:, q % 2, :], tsg[:, q % 2, :], 65536.0, None, ALU.mult).then_inc(si_ready, 1)
                dve.wait_ge(si_ready, q + 1)
                link(V.tensor_tensor(gate_c[:, q * CH:(q + 1) * CH], tgi[:, q % 2, :], tsi[:, q % 2, :], ALU.mult))
                V.tensor_reduce(amax[:, 2, q:q + 1], gate_c[:, q * CH:(q + 1) * CH], AX.X, ALU.max,
                                apply_absolute_value=True).then_inc(p_ready, 1)

            for q in range(NCH):
                gu_maximum(1, 2 * q)
                gu_maximum(1, 2 * q + 1).then_inc(gu_max, 1)
                gate_product(q)
            dve.wait_ge(gu_max, NCH)
            dve.wait_ge(p_ready, NCH)
            scale(2, amax[:, 1, :], s1(4), 13, 12)
            scale(3, amax[:, 2, 0:NCH], s1(14), 15, 16, [(17, s1(15), s1(13))])
            for q in range(NCH):
                dve.wait_ge(pi_ready, q + 1)
                dve.wait_ge(ui_ready, q + 1)
                link(V.tensor_tensor(up_c[:, q * CH:(q + 1) * CH], tpi[:, q % 2, :], tui[:, q % 2, :], ALU.mult))
                V.tensor_reduce(amax[:, 3, q:q + 1], up_c[:, q * CH:(q + 1) * CH], AX.X, ALU.max,
                                apply_absolute_value=True).then_inc(o_ready, 1)
            dve.wait_ge(o_ready, NCH)
            scale(4, amax[:, 3, 0:NCH], s1(17), 18, 19, [(20, s1(18), gates[:, 1:2])])
            dve.wait_ge(scale_ready, 4)

            def finish(t):
                dve.wait_ge(down_done, 2 * t + 2)
                dve.wait_ge(xres_ld[t % 2], 16 * (t // 2 + 1))
                if t >= 2:
                    dve.wait_ge(y_out[t % 2], 16 * (t // 2))
                V.scalar_tensor_tensor(out=yout[:, t % 2, :, :],
                                       in0=bank[2 + t % 4][:, :].rearrange("p (b d) -> p b d", b=2),
                                       scalar=s1(20), in1=xres[:, t % 2, :, :], op0=ALU.mult,
                                       op1=ALU.add).then_inc(y_ready, 1)

            for n in range(4 * KI):
                tg, j = n // KI, n % KI
                if n >= 2:
                    dve.wait_ge(ol_ready, n - 1)
                V.tensor_scalar(tgi[:, n % 2, 0:512], up[:, j, tg * 512:(tg + 1) * 512], s1(19), None,
                                ALU.mult).then_inc(oi_ready, 1)
                dve.wait_ge(oh_ready, n + 1)
                low(oI[1][:, tg % 2, j, :], tgi[:, n % 2, 0:512], oI[0][:, tg % 2, j, :]).then_inc(ol_ready, 1)
                if tg >= 2 and j == 2:
                    finish(2 * tg - 4)
                if tg >= 2 and j == 4:
                    finish(2 * tg - 3)
            for t in range(4, 8):
                finish(t)

        @block.gpsimd
        def _(pool):
            G = nc.gpsimd
            row = lambda a: a.rearrange("(o n) -> o n", o=1)
            G.memset(ident[:, :], 0.0).then_inc(ident_zero, 1)
            pool.wait_ge(ident_zero, 1)
            G.affine_select(out=ident[:, :], in_=ident[:, :], compare_op=ALU.not_equal, fill=1.0, base=0,
                            pattern=[[-1, P]], channel_multiplier=1).then_inc(ident_ready, 1)
            pool.dma_start(gates[:, 0:1], row(g_xattn).to_broadcast([P, 1])).then_inc(const_in, 16)
            pool.dma_start(gates[:, 1:2], row(g_ffn).to_broadcast([P, 1])).then_inc(const_in, 16)
            pool.dma_start(gs[:, :], row(ln_scale).to_broadcast([P, D])).then_inc(const_in, 16)
            pool.dma_start(gb[:, :], row(ln_bias).to_broadcast([P, D])).then_inc(const_in, 16)
            with nc.allow_non_contiguous_dma(reason="one null key and value, 128 numbers"):
                for h in range(2):
                    pool.dma_start(ncol[h * DH:(h + 1) * DH, :], null_kv.rearrange("t d -> d t")).then_inc(const_in, 16)

            def normalise(g, c):
                pool.wait_ge(rinv_done, g * NS + c + 1)
                G.tensor_tensor(probs[:, c % 2, :, 0:S], probs[:, c % 2, :, 0:S],
                                rinv[:, c % 2, :].rearrange("p (u o) -> p u o", o=1).to_broadcast([P, 4, S]),
                                ALU.mult).then_inc(norm_done, 1)
                if c == 0 and not (isinstance(g, int) and g == 0):
                    wait(pool, pt_done, g * (NS + 1))
                G.tensor_tensor(pnull[:, :, 2 * c:2 * c + 2].rearrange("p b h -> p h b"),
                                probs[:, c % 2, :, S].rearrange("p (h b) -> p h b", h=2),
                                rinv[:, c % 2, :].rearrange("p (h b) -> p h b", h=2), ALU.mult).then_inc(pnull_done, 1)

            normalise(0, 0)
            pool.wait_ge(const_ready, 1)

            def group(g):
                for c in range(1, NS):
                    if c == 6:
                        pool.wait_ge(xres_in, 16 * (g + 1))
                        G.tensor_tensor(xr[:, :, :], xr[:, :, :],
                                        gb[:, :].rearrange("p (o d) -> p o d", o=1).to_broadcast([P, GB, D]),
                                        ALU.add).then_inc(xgb_ready, 1)
                    normalise(g, c)
                    if c == 1 and not (isinstance(g, int) and g == 0):
                        pool.wait_ge(w_free, g + 1)
                        G.tensor_tensor(y[:, :, :], y[:, :, :],
                                        gs[:, :].rearrange("p (o d) -> p o d", o=1).to_broadcast([P, GB, D]),
                                        ALU.mult).then_inc(ln_scaled, 1)
                    if c == 2 and not (isinstance(g, int) and g == 0):
                        pool.wait_ge(ln_scaled, g)
                        pool.wait_ge(xgb_ready, g)
                        G.tensor_tensor(y[:, :, :], y[:, :, :], xr[:, :, :], ALU.add).then_inc(x2_ready, 1)
                if not (isinstance(g, int) and g == NG - 1):
                    normalise(g + 1, 0)

            group(0)
            with pool.Fori(1, LOOPED) as g:
                group(g)
            group(NG - 2)
            group(NG - 1)

            gate_c = gate[:, :, :].rearrange("p j t -> p (j t)")
            pool.wait_ge(scale_ready, 1)
            for q in range(NCH):
                if q >= 2:
                    pool.wait_ge(p_ready, q - 1)
                G.tensor_scalar(tgi[:, q % 2, :], gate_c[:, q * CH:(q + 1) * CH], small[:, 11:12], 1.0,
                                ALU.mult, ALU.mult).then_inc(gi_ready, 1)
            pool.wait_ge(scale_ready, 3)
            for q in range(NCH):
                if q >= 2:
                    pool.wait_ge(o_ready, q - 1)
                G.tensor_scalar(tpi[:, q % 2, :], gate_c[:, q * CH:(q + 1) * CH], small[:, 16:17], 1.0,
                                ALU.mult, ALU.mult).then_inc(pi_ready, 1)


_INS = ['x', 'ctx_2048', 'g_xattn', 'g_ffn', 'L0_xattn_Wq', 'L0_xattn_Wkv', 'L0_xattn_null_kv', 'L0_xattn_Wout',
        'L0_xattn_ln_scale', 'L0_xattn_ln_bias', 'L0_ffn_w_gate', 'L0_ffn_w_up', 'L0_ffn_w_down']


def kernel(**inputs):
    import numpy as _np
    import concourse.bacc as _bacc
    from concourse import mybir as _mybir
    from concourse.bass_utils import run_bass_kernel_spmd as _run

    nc = _bacc.Bacc("TRN2", target_bir_lowering=False, num_devices=1)
    arrays, args = {}, []
    for name in _INS:
        a = _np.ascontiguousarray(inputs[name])
        arrays[f"in_{name}"] = a
        args.append(nc.dram_tensor(f"in_{name}", a.shape, _mybir.dt.from_np(a.dtype), kind="ExternalInput").ap())
    shape = arrays["in_x"].shape
    args.append(nc.dram_tensor("out_0", shape, _mybir.dt.float32, kind="ExternalOutput").ap())
    gated_cross_attention_ffn(nc, *args)
    return _run(nc, [arrays], core_ids=[0]).results[0]["out_0"]
```

```python
from contextlib import ExitStack

import concourse.bass as bass
from concourse import mybir

ALU = mybir.AluOpType
ACT = mybir.ActivationFunctionType
AX = mybir.AxisListType
F32 = mybir.dt.float32
F32R = mybir.dt.float32r
I16 = mybir.dt.int16
U16 = mybir.dt.uint16
I32 = mybir.dt.int32

P = 128
EPS_LN = 1e-5
EPS_OUT = 1e-6
QMAX = 32767.0
WMAX = 7.0
WBLOCK = 32
MIN_SCALE = 1e-12
RSQRT_MAGIC = 1597463007.0
NEWTON = 3

TERMS = ((0, 0), (0, 1), (1, 0))


def wait(engine, sem, value):
    if not isinstance(value, int) or value > 0:
        engine.wait_ge(sem, value)


class Chain:

    def __init__(self, engine, sem, per):
        self.engine, self.sem, self.per = engine, sem, per

    def start(self, call, done=0):
        self.base, self.k = call * self.per, done

    def count(self, ins):
        self.k += 1
        ins.then_inc(self.sem, 1)

    def wait(self):
        self.engine.wait_ge(self.sem, self.base + self.k)

    def link(self, ins):
        self.count(ins)
        self.wait()

    def end(self):
        assert self.k == self.per, (self.k, self.per)


def gated_cross_attention_ffn(nc, x, ctx, g_xattn, g_ffn, Wq, Wkv, null_kv, Wout, ln_scale, ln_bias,
                              w_gate, w_up, w_down, out):
    B, S, D = x.shape
    C = ctx.shape[2]
    INNER = Wq.shape[1]
    DH = null_kv.shape[1]
    HEADS = INNER // DH
    I = w_gate.shape[0]
    GB = 2
    NG = B // GB
    TG = GB * S
    KD, KC, KF = D // P, C // P, INNER // P
    NS = KF
    KI = I // P
    NT = B * S // P
    QW = S + 2
    NK = S + 1
    NBK = I * D // P // WBLOCK
    SCALE = float(DH) ** -0.5

    PRO = (["X", "Ca", "q0", "Cb", "q2", "q4", "q6", "k0", "k2", "k4", "k6"] +
           ["V00", "V10", "V01", "V11", "X", "Ca", "Cb", "W"])
    PRO_BEFORE = {2: 1, 3: 1, 4: 2, 5: 1, 6: 2, 7: 1, 8: 1, 9: 1}
    PLAN = ([["Q0"], ["Q1"], ["Q2"], ["Q3"], ["Q4"], ["Q5", "V00"], ["Q6", "V10"], ["Q7", "X"]],
            ["V01", "null", "Ca", "V11", "Cb", "W"])
    PLAN_PENULT = ([["Q0"], ["Q1"], ["Q2"], ["Q3"], ["Q4"], ["V00"], ["Q5"], ["Q6"]], ["null", "V10", "W"])
    PLAN_FINAL = ([["V01"], ["V11"], ["Q7", "F0"], ["F1"], ["F2"], ["F3"], ["F4"], ["F5", "F6"]],
                  ["null", "F7", "F8", "W"])
    BODY, PENULT, FINAL = ([u for step in steps + [tail] for u in step if u != "null"]
                           for steps, tail in (PLAN, PLAN_PENULT, PLAN_FINAL))
    LOOPED = NG - 2

    def units(g):
        if isinstance(g, str):
            return PRO, 0
        if isinstance(g, int) and g == NG - 1:
            return FINAL, len(PRO) + LOOPED * len(BODY) + len(PENULT)
        return (PENULT if isinstance(g, int) and g == LOOPED else BODY), g * len(BODY) + len(PRO)

    def plan(g):
        if isinstance(g, int) and g >= LOOPED:
            return (PLAN_PENULT, PLAN_FINAL)[g - LOOPED]
        return PLAN

    def is_split(kind):
        return kind[0] in "XCF"

    def copied(g, pos):
        first = units(g)[1]
        if isinstance(g, str):
            return pos + 1
        if isinstance(g, int) and g == NG - 1:
            return first - (NG - 1) + pos + 1
        return g * (len(BODY) - 1) + len(PRO) + pos + 1

    def low_made(g, pos):
        if isinstance(g, str):
            return sum(map(is_split, PRO[:pos + 1]))
        before = LOOPED if isinstance(g, int) and g > LOOPED else g
        return before * sum(map(is_split, BODY)) + sum(map(is_split, PRO)) + sum(map(is_split, units(g)[0][:pos + 1]))

    def parity(g, pos):
        if isinstance(g, str) or isinstance(g, int):
            return (units(g)[1] + pos) % 2
        return (len(PRO) + pos) % 2

    def feeds(g):
        return not isinstance(g, int) or g < LOOPED

    x_t = x.rearrange("b s d -> s b d")
    ctx_t = ctx.rearrange("b s d -> s b d")
    out_t = out.rearrange("b s d -> s b d")
    x2_dram = nc.dram_tensor("x2_scratch", (B, S, D), F32, kind="Internal").ap()
    x2_t = x2_dram.rearrange("b s d -> s b d")

    keep, att, ffn = ExitStack(), ExitStack(), ExitStack()
    with keep:
        stack = [keep]

        def sb(name, shape, dt=F32):
            return stack[0].enter_context(nc.sbuf_tensor(name, shape, dt))

        def sem(name):
            return keep.enter_context(nc.semaphore(name))

        ident = sb("ident", [P, P])
        ones = sb("ones", [1, P])
        gates = sb("gates", [P, 2])
        mean_var = sb("mean_var", [P, NT, 2])
        x2_max = sb("x2_max", [P, NT])
        x2_min = sb("x2_min", [P, NT])
        pause = sb("pause", [P, 1])
        spare = sb("spare", [P, 1])
        small = sb("small", [P, 32])

        stack[0] = att
        wv = [sb(f"wv{i}", [P, KC, INNER], F32R) for i in range(2)]
        craw = sb("craw", [P, GB, C])
        wk = [sb(f"wk{i}", [P, KC, INNER], F32R) for i in range(2)]
        wq = [sb(f"wq{i}", [P, KD, INNER], F32R) for i in range(2)]
        wout = [sb(f"wout{i}", [P, KF, D], F32R) for i in range(2)]
        fraw = sb("fraw", [P, 3, NBK, WBLOCK])
        fint = sb("fint", [P, NBK, WBLOCK], I16)
        fs = sb("fs", [P, 2, NBK])
        qk = sb("qk", [P, NS, 2 * GB, QW])
        v = sb("v", [P, GB, NS, P])
        xnT = [sb(f"xnT{i}", [P, KD, TG], F32R) for i in range(2)]
        ctxT = [sb(f"ctxT{i}", [P, KC, TG], F32R) for i in range(2)]
        wnull = [sb(f"wnull{i}", [HEADS, D], F32R) for i in range(2)]
        nullT = [sb(f"nullT{i}", [HEADS, TG], F32R) for i in range(2)]
        gs = sb("gs", [P, D])
        gb = sb("gb", [P, D])
        nmax = sb("nmax", [P, 2, 4])
        rowsum = sb("rowsum", [P, 2, 4])
        rinv = sb("rinv", [P, 2, 4])
        pnull = sb("pnull", [P, GB, HEADS])
        bn = sb("bn", [P, 4, 6])
        mv = sb("mv", [P, 4, 2])
        rs = sb("rs", [P, 8, 2])
        xa = sb("xa", [P, GB, D])
        xr = sb("xr", [P, GB, D])
        y = sb("y", [P, GB, D])
        late = ExitStack()
        stack[0] = late
        probs = sb("probs", [P, 2, 4, QW])
        pT = sb("pT", [P, 2, 4, P])
        oT = [sb(f"oT{i}", [P, KF, TG], F32R) for i in range(2)]
        late.close()
        stack[0] = late = ExitStack()
        NST = 7
        STW = 1024
        stage = sb("stage", [P, NST, STW])
        nkw = sb("nkw", [P, NS * GB, 2])
        nvm = sb("nvm", [P, KF, HEADS])
        nvr = [sb(f"nvr{i}", [P, KF, HEADS], F32R) for i in range(2)]
        ncol = sb("ncol", [P, 2])
        late.close()
        att.close()

        CH = 1024
        NCH = KI * B * S // CH
        HC = CH // 2
        GS = 6
        stack[0] = ffn
        early = ExitStack()
        stack[0] = early
        wg = [sb(f"wg{i}", [P, KD, I], F32R) for i in range(2)]
        wu = [sb(f"wu{i}", [P, KD, I], F32R) for i in range(2)]
        early.close()
        stack[0] = ffn
        oI = [sb("oI0", [P, 2, KI, 512], F32R)]
        wd = [sb(f"wd{i}", [P, KI, D], F32R) for i in range(2)]
        early = ExitStack()
        stack[0] = early
        x2all = sb("x2all", [P, NT, D])
        early.close()
        stack[0] = ffn
        up = sb("up", [P, KI, B * S])
        early = ExitStack()
        stack[0] = early
        oI.append(sb("oI1", [P, 2, KI, 512], F32R))
        early.close()
        early = ExitStack()
        stack[0] = early
        oI1_place = sb("oI1_place", [P, 2, KI, 512])
        xlast = sb("xlast", [P, 2, 2, D])
        early.close()
        early = ExitStack()
        stack[0] = early
        prod = sb("prod", [P, 2, CH])
        early.close()
        stack[0] = ffn
        xT = [sb(f"xT{i}", [P, KD, B * S], F32R) for i in range(2)]
        gate = sb("gate", [P, KI, B * S])
        tgi = sb("tgi", [P, GS, HC], I16)
        tsi = sb("tsi", [P, GS, HC], U16)
        tui = sb("tui", [P, 4, CH], I16)
        early = ExitStack()
        stack[0] = early
        tsg = sb("tsg", [P, 4, HC])
        early.close()
        stack[0] = ffn
        tpi = sb("tpi", [P, 4, CH], I16)
        xi = sb("xi", [P, 2, 2, D], I16)
        early = ExitStack()
        stack[0] = early
        xf = sb("xf", [P, 2, 2, D])
        early.close()
        stack[0] = ffn
        yout = sb("yout", [P, 2, 2, D])
        xres = sb("xres", [P, 2, 2, D])
        fa = sb("fa", [P, 4, NT])
        rs3 = sb("rs3", [P, 4, NT])
        amax = sb("amax", [P, 4, 2 * 4 * KI])
        ffn.close()

        bank = [keep.enter_context(nc.psum_tensor(f"bank{i}", [P, 512], F32)) for i in range(8)]
        score_bank = [[bank[0], bank[1]], [bank[2], bank[3]]]
        pt_bank, pv_bank = bank[4], bank[5]
        unit_bank = [bank[6], bank[7]]

        stage_in = [sem(f"stage_in{i}") for i in range(NST)]
        wsplit_hi, wsplit_lo = sem("wsplit_hi"), sem("wsplit_lo")
        const_in, const_ready, null_ready = sem("const_in"), sem("const_ready"), sem("null_ready")
        ident_ready, ident_zero, tanh_done = sem("ident_ready"), sem("ident_zero"), sem("tanh_done")
        x_in, ctx_in, xres_in, x2_out = sem("x_in"), sem("ctx_in"), sem("xres_in"), sem("x2_out")
        xn_ready = sem("xn_ready")
        unit_done, unit_hi, unit_lo, w_free = sem("unit_done"), sem("unit_hi"), sem("unit_lo"), sem("w_free")
        scores_done, max_done, exp_done = sem("scores_done"), sem("max_done"), sem("exp_done")
        rinv_done, norm_done, pnull_done = sem("rinv_done"), sem("norm_done"), sem("pnull_done")
        pt_done, pt_copied, null_hi = sem("pt_done"), sem("pt_copied"), sem("null_hi")
        pv_done, ot_hi, ot_lo = sem("pv_done"), sem("ot_hi"), sem("ot_lo")
        ln1_chain, ln2_chain, ln3_chain = sem("ln1_chain"), sem("ln2_chain"), sem("ln3_chain")
        prep_chain, fchain = sem("prep_chain"), sem("fchain")
        xgb_ready, x2_ready, x2_stats = sem("xgb_ready"), sem("x2_ready"), sem("x2_stats")
        fraw_in = [sem(f"fraw_in{i}") for i in range(3)]
        fint_ready, fw_ready = sem("fint_ready"), sem("fw_ready")
        gm_t, gm_1, gm_b, scale_ready = sem("gm_t"), sem("gm_1"), sem("gm_b"), sem("scale_ready")
        x2all_in, xaffine, xi_first, xi_ready = sem("x2all_in"), sem("xaffine"), sem("xi_first"), sem("xi_ready")
        xf_ready, xt_done, xt_hi, xt_lo = sem("xf_ready"), sem("xt_done"), sem("xt_hi"), sem("xt_lo")
        gu_done, gu_out, gu_max = sem("gu_done"), sem("gu_out"), sem("gu_max")
        gi_ready, sg_ready, si_ready, p_ready = sem("gi_ready"), sem("sg_ready"), sem("si_ready"), sem("p_ready")
        pi_scalar, pi_pool, ui_ready, o_ready = sem("pi_scalar"), sem("pi_pool"), sem("ui_ready"), sem("o_ready")
        ti_ready, tu_ready, oi_ready = sem("ti_ready"), sem("tu_ready"), sem("oi_ready")
        oh_ready, ol_ready = sem("oh_ready"), sem("ol_ready")
        down_done, fin_scaled, y_ready, y_last = sem("down_done"), sem("fin_scaled"), sem("y_ready"), sem("y_last")
        xres_ld = [sem(f"xres_ld{i}") for i in range(2)]
        y_out = [sem(f"y_out{i}") for i in range(2)]
        y_out_last, xlast_in = sem("y_out_last"), sem("xlast_in")

        block = keep.enter_context(nc.Block())

        wq_r = Wq.rearrange("(k p) f -> p k f", p=P)
        wkv_r = Wkv.rearrange("(k p) f -> p k f", p=P)
        wout_r = Wout.rearrange("(k p) f -> p k f", p=P)
        pieces = [([w[:, k, :] for w in wq], wq_r[:, k, :], SCALE, None) for k in range(KD)]
        pieces += [([w[:, k, :] for w in wk], wkv_r[:, k, 0:INNER], 1.0, None) for k in range(KC)]
        pieces += [([w[:, k, :] for w in wv], wkv_r[:, k, INNER:], 1.0, None) for k in range(KC)]
        pieces += [([w[:, 4 * j:4 * j + 4, :] for w in wout], wout_r[:, 4 * j:4 * j + 4, :], 1.0, 4) for j in range(2)]
        NPC = len(pieces)
        READY_Q, READY_K, READY_V = KD, KD + KC, KD + 2 * KC

        def stage_view(i, fold):
            s = stage[:, i % NST, :]
            return s if fold is None else s.rearrange("p (a b) -> p a b", a=fold)

        fw_r = [w.rearrange("(j p) h -> p j h", p=P) for w in (w_gate, w_up, w_down)]

        def unit_view(kind, hl):
            if kind[0] == "Q":
                return qk[:, int(kind[1]), :, 0:S]
            if kind[0] in "qk":
                c, a = int(kind[1]), GB * "qk".index(kind[0])
                return qk[:, c:c + 2, a:a + GB, 0:S]
            if kind[0] == "V":
                b, h = int(kind[1]), int(kind[2])
                return v[:, b, 4 * h:4 * h + 4, :].rearrange("p c d -> p (c d)")
            if kind == "X":
                return xnT[hl][:, :, :]
            if kind[0] == "C":
                b = "ab".index(kind[1])
                return ctxT[hl][:, :, b * S:(b + 1) * S]
            i = int(kind[1])
            m, r = i // 3, i % 3
            if m < 2:
                return (wg, wu)[m][hl][:, :, 2 * r * P:(2 * r + 2) * P]
            return wd[hl][:, 2 * r:2 * r + 2, :]

        def unit_psum(kind, bk):
            if kind[0] == "Q":
                return bk[:, :].rearrange("p (a s) -> p a s", s=S)
            if kind[0] in "qk":
                return bk[:, :].rearrange("p (c a s) -> p c a s", c=2, s=S)
            if kind[0] == "V":
                return bk[:, :]
            if kind[0] == "C":
                return bk[:, :].rearrange("p (a s) -> p a s", s=S)
            return bk[:, :].rearrange("p (a s) -> p a s", s=2 * P)

        def gate_piece(n):
            return gate[:, n % KI, n // KI * HC:(n // KI + 1) * HC]

        def by_vector(q):
            return q % 6 == 5

        def pool_made(q):
            return sum(not by_vector(i) for i in range(q + 1))

        def magnitude_by_scalar(q):
            return q % 3 != 0

        def up_piece(n):
            return up[:, n % KI, n // KI * HC:(n // KI + 1) * HC]

        def ui(n):
            return tui[:, n % 4 // 2, n % 2 * HC:(n % 2 + 1) * HC]

        def oint(n):
            return tui[:, 2 + n % 4 // 2, n % 2 * HC:(n % 2 + 1) * HC]

        @block.sync
        def _(sp):
            sp.dma_start(xa[:, :, :], x_t[:, 0:GB, :]).then_inc(x_in, 16)
            for i, (_, src, _, fold) in enumerate(pieces):
                if i >= NST:
                    sp.wait_ge(wsplit_lo, i - NST + 1)
                sp.dma_start(stage_view(i, fold), src).then_inc(stage_in[i % NST], 16)
                if i == READY_Q - 1:
                    sp.dma_start(craw[:, :, :], ctx_t[:, 0:GB, :]).then_inc(ctx_in, 16)
                if i == 6:
                    sp.wait_ge(unit_done, 1)
                    sp.dma_start(xa[:, :, :], x_t[:, GB:2 * GB, :]).then_inc(x_in, 16)
                if i == 7:
                    sp.wait_ge(unit_done, PRO.index("Cb") + 1)
                    sp.dma_start(craw[:, :, :], ctx_t[:, GB:2 * GB, :]).then_inc(ctx_in, 16)

            for m in range(3):
                sp.dma_start(fraw[:, m, :, :].rearrange("p n w -> p (n w)").rearrange(
                    "p (j h) -> p j h", j=(KI, KI, 2)[m]), fw_r[m]).then_inc(fraw_in[m], 16)

            def group_dma(g):
                if feeds(g):
                    sp.wait_ge(unit_done, g * len(BODY) + len(PRO) - 3)
                    sp.dma_start(xa[:, :, :], x_t[:, bass.ds((g + 2) * GB, GB), :]).then_inc(x_in, 16)
                    sp.wait_ge(unit_done, g * len(BODY) + len(PRO) - 1)
                    sp.dma_start(craw[:, :, :], ctx_t[:, bass.ds((g + 2) * GB, GB), :]).then_inc(ctx_in, 16)
                if not (isinstance(g, int) and g == 0):
                    sp.wait_ge(x2_ready, g)
                    sp.dma_start(x2_t[:, bass.ds((g - 1) * GB, GB), :], y[:, :, :]).then_inc(x2_out, 16)
                sp.dma_start(xr[:, :, :], x_t[:, bass.ds(g * GB, GB), :]).then_inc(xres_in, 16)

            group_dma(0)
            with sp.Fori(1, LOOPED) as g:
                group_dma(g)
            group_dma(NG - 2)
            group_dma(NG - 1)
            sp.wait_ge(unit_done, units(NG - 1)[1] + FINAL.index("Q7") + 1)
            sp.wait_ge(x2_out, 16 * (NG - 1))
            sp.dma_start(x2all[:, 0:(NG - 1) * GB, :], x2_t[:, 0:(NG - 1) * GB, :]).then_inc(x2all_in, 16)
            sp.wait_ge(x2_ready, NG)
            sp.dma_start(x2_t[:, (NG - 1) * GB:, :], x2all[:, (NG - 1) * GB:, :]).then_inc(x2_out, 16)
            sp.wait_ge(x2_out, 16 * NG)
            sp.wait_ge(xi_ready, NT // 2 - 1)

            def load_residual(t):
                sp.dma_start(xres[:, t % 2, :, :], x2_t[:, 2 * t:2 * t + 2, :]).then_inc(xres_ld[t % 2], 16)

            load_residual(0)
            load_residual(1)
            sp.wait_ge(gu_out, 8 * KI)
            sp.dma_start(xlast[:, :, :, :].rearrange("p t b d -> p (t b) d"),
                         x2_t[:, NT - 4:, :]).then_inc(xlast_in, 16)
            for t in range(NT // 2):
                o = out_t[:, 2 * t:2 * t + 2, :]
                if t < 6:
                    sp.wait_ge(y_ready, t + 1)
                    sp.dma_start(o, yout[:, t % 2, :, :]).then_inc(y_out[t % 2], 16)
                else:
                    sp.wait_ge(y_last, t - 5)
                    sp.dma_start(o, xlast[:, t % 2, :, :]).then_inc(y_out_last, 16)
                if t + 2 < NT // 2 - 2:
                    load_residual(t + 2)
            for i in range(2):
                sp.wait_ge(y_out[i], 16 * 3)
            sp.wait_ge(y_out_last, 16 * 2)

        @block.tensor
        def _(pe):
            mm = nc.tensor.matmul

            def unit_read(g, pos):
                if is_split(units(g)[0][pos]):
                    pe.wait_ge(unit_lo, low_made(g, pos))
                else:
                    pe.wait_ge(unit_hi, copied(g, pos))

            def unit(g, pos):
                seq = units(g)[0]
                kind, bk = seq[pos], unit_bank[parity(g, pos)]
                if pos >= 2:
                    unit_read(g, pos - 2)
                elif pos == 1 and not isinstance(g, str):
                    pe.wait_ge(w_free, g + 1)
                elif pos == 0 and isinstance(g, int) and g == NG - 1:
                    unit_read(g - 1, len(PENULT) - 2)
                elif not isinstance(g, str):
                    pe.wait_ge(unit_lo, low_made(g, -1))
                if kind[0] in "qk":
                    if kind == "q0":
                        unit_read(g, PRO.index("X"))
                        pe.wait_ge(wsplit_lo, READY_Q)
                    if kind == "k0":
                        unit_read(g, PRO.index("Cb"))
                        pe.wait_ge(wsplit_lo, READY_K)
                    wt, act_t, kk = (wq, xnT, KD) if kind[0] == "q" else (wk, ctxT, KC)
                    for n in range(2):
                        c = int(kind[1]) + n
                        for k in range(kk):
                            for i, (a, b) in enumerate(TERMS):
                                last = mm(bk[:, n * TG:(n + 1) * TG], wt[a][:, k, c * P:(c + 1) * P],
                                          act_t[b][:, k, :],
                                          start=(k == 0 and i == 0), stop=(k == kk - 1 and i == len(TERMS) - 1))
                elif kind[0] == "Q":
                    c = int(kind[1])
                    if c == 0:
                        pe.wait_ge(unit_lo, low_made(g, -1))
                    f = slice(c * P, (c + 1) * P)
                    for n, (wt, act_t, kk) in enumerate(((wq, xnT, KD), (wk, ctxT, KC))):
                        for k in range(kk):
                            for i, (a, b) in enumerate(TERMS):
                                last = mm(bk[:, n * TG:(n + 1) * TG], wt[a][:, k, f], act_t[b][:, k, :],
                                          start=(k == 0 and i == 0), stop=(k == kk - 1 and i == len(TERMS) - 1))
                elif kind[0] == "V":
                    b, h = int(kind[1]), int(kind[2])
                    if isinstance(g, str) and pos == PRO.index("V00"):
                        pe.wait_ge(wsplit_lo, READY_V)
                    for k in range(KC):
                        for i, (a, w) in enumerate(TERMS):
                            last = mm(bk[:, :], ctxT[a][:, k, b * S:(b + 1) * S],
                                      wv[w][:, k, h * 512:(h + 1) * 512],
                                      start=(k == 0 and i == 0), stop=(k == KC - 1 and i == len(TERMS) - 1))
                elif kind == "X":
                    n = (0 if pos == 0 else 1) if isinstance(g, str) else g + 2
                    if isinstance(g, str) and pos == 0:
                        pe.wait_ge(ident_ready, 1)
                    pe.wait_ge(xn_ready, n + 1)
                    for k in range(KD):
                        for b in range(GB):
                            last = nc.tensor.transpose(bk[:, k * TG + b * S:k * TG + (b + 1) * S],
                                                       xa[:, b, k * P:(k + 1) * P], ident[:, :])
                elif kind[0] == "C":
                    b = "ab".index(kind[1])
                    n = (0 if pos < 3 else 1) if isinstance(g, str) else g + 2
                    if b == 0:
                        pe.wait_ge(ctx_in, (n + 1) * 16)
                    for k in range(KC):
                        last = nc.tensor.transpose(bk[:, k * S:(k + 1) * S], craw[:, b, k * P:(k + 1) * P],
                                                   ident[:, :])
                elif kind[0] == "F":
                    i = int(kind[1])
                    m, r = i // 3, i % 3
                    if r == 0:
                        pe.wait_ge(fw_ready, m + 1)
                    wf = fraw[:, m, :, :].rearrange("p n w -> p (n w)")
                    for a in range(2):
                        for b in range(2):
                            src = ((2 * r + b) * D + a * P) if m < 2 else (b * I + (2 * r + a) * P)
                            last = nc.tensor.transpose(bk[:, (2 * a + b) * P:(2 * a + b + 1) * P],
                                                       wf[:, src:src + P], ident[:, :])
                elif isinstance(g, str):
                    pe.wait_ge(null_ready, 2)
                    pe.wait_ge(wsplit_lo, NPC)
                    for k in range(KF):
                        for i, (a, w) in enumerate(TERMS):
                            last = mm(bk[0:HEADS, 0:D], nvr[a][:, k, :], wout[w][:, k, :],
                                      start=(k == 0 and i == 0), stop=(k == KF - 1 and i == len(TERMS) - 1))
                else:
                    wait(pe, ot_lo, g * NS + NS)
                    wait(pe, pt_copied, g * (NS + 1) + NS + 1)
                    pe.wait_ge(w_free, g + 1)
                    for b in range(GB):
                        o = bk[:, b * D:(b + 1) * D]
                        for k in range(KF):
                            for i, (a, w) in enumerate(TERMS):
                                mm(o, oT[a][:, k, b * S:(b + 1) * S], wout[w][:, k, :],
                                   start=(k == 0 and i == 0), stop=False)
                        for i, (a, w) in enumerate(TERMS):
                            last = mm(o, nullT[a][:, b * S:(b + 1) * S], wnull[w][:, :],
                                      start=False, stop=(i == len(TERMS) - 1))
                last.then_inc(unit_done, 1)

            def scores(g, c):
                if isinstance(g, int) and g == NG - 1 and f"Q{c}" in FINAL:
                    unit_read(g, FINAL.index(f"Q{c}"))
                wait(pe, exp_done, g * NS + c - 1)
                for b in range(GB):
                    for h in range(2):
                        rows = slice(h * DH, (h + 1) * DH)
                        last = mm(score_bank[c % 2][h][:, b * QW:b * QW + QW], qk[rows, c, b, 0:S],
                                  qk[rows, c, GB + b, 0:QW], start=True, stop=True)
                last.then_inc(scores_done, 1)

            def prob_transposes(g, c):
                pe.wait_ge(norm_done, g * NS + c + 1)
                wait(pe, pt_copied, g * (NS + 1) + c)
                for u in range(4):
                    last = nc.tensor.transpose(pt_bank[:, u * P:(u + 1) * P], probs[:, c % 2, u, 0:S], ident[:, :])
                last.then_inc(pt_done, 1)

            def null_transposes(g):
                wait(pe, pnull_done, g * NS + NS)
                wait(pe, pt_copied, g * (NS + 1) + NS)
                for b in range(GB):
                    last = nc.tensor.transpose(pt_bank[0:HEADS, b * S:(b + 1) * S], pnull[:, b, :], ident[:, :])
                last.then_inc(pt_done, 1)

            def values(g, c):
                wait(pe, pt_copied, g * (NS + 1) + c + 1)
                wait(pe, ot_lo, g * NS + c)
                for b in range(GB):
                    for h in range(2):
                        rows = slice(h * DH, (h + 1) * DH)
                        last = mm(pv_bank[rows, b * S:(b + 1) * S], v[:, b, c, rows],
                                  pT[:, c % 2, 2 * h + b, :], start=True, stop=True)
                last.then_inc(pv_done, 1)

            for pos in range(len(PRO)):
                unit("pro", pos)
                if PRO[pos] == "k6":
                    pe.wait_ge(null_ready, 1)
                    scores(0, 0)

            def group(g):
                final = isinstance(g, int) and g == NG - 1
                pos, (steps, tail) = 0, plan(g)
                for c in range(NS):
                    if c + 1 < NS:
                        scores(g, c + 1)
                    for _ in steps[c]:
                        unit(g, pos)
                        pos += 1
                    prob_transposes(g, c)
                    if c:
                        values(g, c - 1)
                if not final:
                    scores(g + 1, 0)
                values(g, NS - 1)
                for u in tail:
                    if u == "null":
                        null_transposes(g)
                    else:
                        unit(g, pos)
                        pos += 1

            group(0)
            with pe.Fori(1, LOOPED) as g:
                group(g)
            group(NG - 2)
            group(NG - 1)

            def global_max(n):
                pe.wait_ge(gm_t, 2 * n + 1)
                nc.tensor.transpose(bank[0][0:1, 0:P], small[:, 0:1], ident[:, :]).then_inc(gm_1, 1)
                pe.wait_ge(gm_t, 2 * n + 2)
                mm(bank[1][:, 0:1], ones[:, :], small[0:1, 1:2], start=True, stop=True).then_inc(gm_b, 1)

            def x_transposes(t):
                pe.wait_ge(xf_ready, t + 1)
                if t >= 2:
                    pe.wait_ge(xt_lo, t - 1)
                for k in range(KD):
                    for b in range(2):
                        last = nc.tensor.transpose(unit_bank[t % 2][:, (2 * k + b) * P:(2 * k + b + 1) * P],
                                                   xf[:, t % 2, b, k * P:(k + 1) * P], ident[:, :])
                last.then_inc(xt_done, 1)

            global_max(0)
            for t in range(2):
                x_transposes(t)
            for m in range(2):
                for tg in range(4):
                    for j in range(KI):
                        n = (m * 4 + tg) * KI + j
                        if m == 0 and j == 0:
                            pe.wait_ge(xt_lo, 2 * tg + 2)
                        bk = bank[2 + n % 4]
                        if n >= 4:
                            pe.wait_ge(gu_out, n - 3)
                        for k in range(KD):
                            for i, (a, w) in enumerate(TERMS):
                                last = mm(bk[:, :], (wg, wu)[m][a][:, k, j * P:(j + 1) * P],
                                          xT[w][:, k, tg * 512:(tg + 1) * 512],
                                          start=(k == 0 and i == 0), stop=(k == KD - 1 and i == len(TERMS) - 1))
                        last.then_inc(gu_done, 1)
                        if m == 0 and tg == 0 and j in (1, 3):
                            x_transposes(2 + j // 2)
                        if m == 1 and tg == 0 and j == 1:
                            global_max(1)
                    if m == 0 and tg < 2:
                        x_transposes(2 * tg + 4)
                        x_transposes(2 * tg + 5)
            for n in range(2, 5):
                global_max(n)
            for tg in range(4):
                for j in range(KI):
                    pe.wait_ge(ol_ready, tg * KI + j + 1)
                    if tg >= 2 and j == 0:
                        pe.wait_ge(fin_scaled, 2 * (tg - 1))
                    for t in range(4):
                        for i, (a, w) in enumerate(TERMS):
                            last = mm(bank[tg % 2 * 4 + t][:, 0:D], oI[a][:, tg % 2, j, t * P:(t + 1) * P],
                                      wd[w][:, j, :], start=(j == 0 and i == 0), stop=(j == KI - 1 and i == 2))
                        if j == KI - 1:
                            last.then_inc(down_done, 1)

        @block.scalar
        def _(act):
            act_copy = ACT.Copy

            def high(dst, src, scale=1.0):
                return nc.scalar.activation(dst, src, act_copy, scale=scale)

            def split(g, pos):
                seq, first = units(g)
                kind = seq[pos]
                if kind == "W" and not isinstance(g, str):
                    return
                act.wait_ge(unit_done, first + pos + 1)
                if kind == "W":
                    high(wnull[0][:, :], unit_bank[parity(g, pos)][0:HEADS, 0:D]).then_inc(unit_hi, 1)
                else:
                    high(unit_view(kind, 0), unit_psum(kind, unit_bank[parity(g, pos)])).then_inc(unit_hi, 1)

            def exps(g, c):
                act.wait_ge(max_done, g * NS + c + 1)
                if not (isinstance(g, int) and g == 0 and c < 2):
                    if c == 0:
                        wait(act, pt_done, g * (NS + 1) - 2)
                    else:
                        wait(act, pt_done, g * (NS + 1) + (c - 1 if c > 1 else 0))
                    wait(act, pnull_done, g * NS + c - 1)
                for u in range(4):
                    h, b = u // 2, u % 2
                    last = nc.scalar.activation(probs[:, c % 2, u, 0:NK],
                                                score_bank[c % 2][h][:, b * QW:b * QW + NK], ACT.Exp,
                                                bias=nmax[:, c % 2, u:u + 1], accum_out=rowsum[:, c % 2, u:u + 1])
                last.then_inc(exp_done, 1)

            def out_high(g, c):
                wait(act, pv_done, g * NS + c + 1)
                high(oT[0][:, c, :], pv_bank[:, 0:TG]).then_inc(ot_hi, 1)

            npos = [0]
            for i, (dst, _, f, fold) in enumerate(pieces):
                for _ in range(PRO_BEFORE.get(i, 0)):
                    split("pro", npos[0])
                    npos[0] += 1
                if i == READY_K:
                    act.wait_ge(const_in, 16 * 6)
                    nc.scalar.activation(gates[:, :], gates[:, :], ACT.Tanh).then_inc(tanh_done, 1)
                act.wait_ge(stage_in[i % NST], 16 * (i // NST + 1))
                high(dst[0], stage_view(i, fold), f).then_inc(wsplit_hi, 1)
            while npos[0] < len(PRO):
                split("pro", npos[0])
                if PRO[npos[0]] == "k6":
                    exps(0, 0)
                npos[0] += 1

            def group(g):
                final = isinstance(g, int) and g == NG - 1
                pos, (steps, tail) = 0, plan(g)
                for c in range(NS):
                    weights = steps[c][0][0:1] == "F"
                    if c + 1 < NS and not weights:
                        exps(g, c + 1)
                    for _ in steps[c]:
                        split(g, pos)
                        pos += 1
                    if c + 1 < NS and weights:
                        exps(g, c + 1)
                    if c:
                        out_high(g, c - 1)
                if not final:
                    exps(g + 1, 0)
                out_high(g, NS - 1)
                for u in tail:
                    if u == "null":
                        wait(act, pt_done, g * (NS + 1) + NS + 1)
                        high(nullT[0][:, :], pt_bank[0:HEADS, 0:TG]).then_inc(null_hi, 1)
                    else:
                        split(g, pos)
                        pos += 1

            group(0)
            with act.Fori(1, LOOPED) as g:
                group(g)
            group(NG - 2)
            group(NG - 1)

            def x_float(t):
                act.wait_ge(xi_ready if t else xi_first, max(t, 1))
                if t >= 2:
                    act.wait_ge(xt_done, t - 1)
                high(xf[:, t % 2, :, :], xi[:, t % 2, :, :]).then_inc(xf_ready, 1)

            def x_high(t):
                act.wait_ge(xt_done, t + 1)
                high(xT[0][:, :, t * TG:(t + 1) * TG],
                     unit_bank[t % 2][:, :].rearrange("p (k s) -> p k s", k=KD)).then_inc(xt_hi, 1)

            def gu(m, n):
                tg, j = n // KI, n % KI
                q = m * 4 * KI + n
                act.wait_ge(gu_done, q + 1)
                nc.scalar.activation((gate, up)[m][:, j, tg * 512:(tg + 1) * 512], bank[2 + q % 4][:, :],
                                     act_copy).then_inc(gu_out, 1)

            x_float(0)
            for t in range(1, 3):
                x_float(t)
                x_high(t - 1)
            x_float(3)
            for tg in range(4):
                for j in range(KI):
                    gu(0, tg * KI + j)
                    if tg == 0 and j in (1, 3):
                        x_high(2 + j // 2)
                    if tg < 2 and j in (2, 4):
                        x_float(2 * tg + 3 + j // 2)
                if tg < 2:
                    x_high(2 * tg + 4)
                    x_high(2 * tg + 5)
            act.wait_ge(gu_out, 1)
            nc.scalar.activation(spare[:, :], small[:, 4:5], ACT.Sigmoid)
            gate_c = gate[:, :, :].rearrange("p j t -> p (j t)")
            up_c = up[:, :, :].rearrange("p j t -> p (j t)")
            act.wait_ge(x2_out, 16 * NG)

            def sigmoid(q):
                n = HC if q < 4 * KI else 1
                act.wait_ge(gi_ready, q + 1)
                if q >= 4 and by_vector(q - 4):
                    act.wait_ge(p_ready, q - 3)
                elif q >= 4:
                    act.wait_ge(si_ready, pool_made(q - 4))
                nc.scalar.activation(tsg[:, q % 4, 0:n], tgi[:, q % GS, 0:n], ACT.Sigmoid,
                                     scale=small[:, 10:11]).then_inc(sg_ready, 1)

            for q in range(4):
                gu(1, q)
            for q in range(4 * KI + 1):
                sigmoid(q)
                if q + 4 < 4 * KI:
                    gu(1, q + 4)

            act.wait_ge(scale_ready, 2)
            for q in range(4):
                nc.scalar.activation(tui[:, q, :], up_c[:, q * CH:(q + 1) * CH], ACT.Abs,
                                     scale=small[:, 12:13]).then_inc(ui_ready, 1)
            act.wait_ge(scale_ready, 3)
            for q in range(NCH):
                if q >= 4:
                    act.wait_ge(o_ready, q - 3)
                if magnitude_by_scalar(q):
                    nc.scalar.activation(tpi[:, q % 4, :], gate_c[:, q * CH:(q + 1) * CH], ACT.Abs,
                                         scale=small[:, 16:17]).then_inc(pi_scalar, 1)
                if q >= 4:
                    nc.scalar.activation(tui[:, q % 4, :], up_c[:, q * CH:(q + 1) * CH], ACT.Abs,
                                         scale=small[:, 12:13]).then_inc(ui_ready, 1)

            def up_integers(n):
                if n >= 4:
                    act.wait_ge(oi_ready, n - 3)
                nc.scalar.activation(ui(n), up_piece(n), act_copy, scale=small[:, 12:13]).then_inc(tu_ready, 1)

            def finish(t):
                act.wait_ge(down_done, 2 * t + 2)
                if t >= 2:
                    act.wait_ge(y_out[t % 2], 16 * (t // 2))
                for b in range(2):
                    last = high(yout[:, t % 2, b, :], bank[(2 * t + b) % 8][:, 0:D], small[:, 20:21])
                last.then_inc(fin_scaled, 1)

            act.wait_ge(o_ready, NCH)
            for n in range(3):
                up_integers(n)
            act.wait_ge(scale_ready, 5)
            for n in range(4 * KI):
                if n + 3 < 4 * KI:
                    up_integers(n + 3)
                act.wait_ge(oi_ready, n + 1)
                tg, j = n // KI, n % KI
                if tg >= 2 and j == 0:
                    act.wait_ge(down_done, 4 * (tg - 1))
                high(oI[0][:, tg % 2, j, :], oint(n)).then_inc(oh_ready, 1)
                if tg >= 2 and j in (1, 3):
                    finish(2 * tg - 4 + j // 2)
            for t in range(4, 6):
                finish(t)

        @block.vector
        def _(dve):
            V = nc.vector

            def low(dst, src, hi, f=1.0):
                if f == 1.0:
                    return V.tensor_tensor(dst, src, hi.bitcast(F32), ALU.subtract)
                return V.scalar_tensor_tensor(out=dst, in0=src, scalar=f, in1=hi.bitcast(F32), op0=ALU.mult,
                                              op1=ALU.subtract)

            def rsqrt_start(link, var, r, eps):
                link(V.tensor_scalar(r[1], var, eps, None, ALU.add))
                link(V.tensor_scalar(r[0].bitcast(I32), r[1].bitcast(I32), -0.5, RSQRT_MAGIC, ALU.mult, ALU.add))
                newton(link, r)

            def newton(link, r):
                link(V.scalar_tensor_tensor(out=r[2], in0=r[0], scalar=-0.5, in1=r[0], op0=ALU.mult, op1=ALU.mult))
                link(V.tensor_tensor(r[2], r[2], r[1], ALU.mult))
                link(V.scalar_tensor_tensor(out=r[0], in0=r[2], scalar=1.5, in1=r[0], op0=ALU.add, op1=ALU.mult))

            def rsqrt_end(link, r):
                for _ in range(NEWTON - 1):
                    newton(link, r)

            def settle():
                V.memset(pause[:, :], 0.0)

            NRS = 2 + 3 * NEWTON
            ln1 = Chain(dve, ln1_chain, 2 + NRS)
            ln2 = Chain(dve, ln2_chain, 2 + NRS)
            ln3 = Chain(dve, ln3_chain, 2)

            def ln_stats(n):
                dve.wait_ge(x_in, (n + 1) * 16)
                ln1.start(n)
                for b in range(GB):
                    last = V.bn_stats(bn[:, b, :], xa[:, b, :])
                ln1.link(last)
                settle()
                for b in range(GB):
                    last = V.bn_aggr(mv[:, b, :], bn[:, b, :])
                ln1.link(last)

            def ln_rstd():
                r = [rs[:, i, :] for i in range(3)]
                rsqrt_start(ln1.link, mv[:, 0:2, 1], r, EPS_LN)
                rsqrt_end(ln1.link, r)
                ln1.end()

            def ln_apply():
                for b in range(GB):
                    last = V.tensor_scalar(xa[:, b, :], xa[:, b, :], mv[:, b, 0:1], rs[:, 0, b:b + 1],
                                           ALU.subtract, ALU.mult)
                last.then_inc(xn_ready, 1)

            def split(g, pos):
                kind = units(g)[0][pos]
                bk = unit_bank[parity(g, pos)]
                if kind == "W" and isinstance(g, str):
                    dve.wait_ge(unit_hi, copied(g, pos))
                    low(wnull[1][:, :], bk[0:HEADS, 0:D], wnull[0][:, :]).then_inc(w_free, 1)
                elif is_split(kind):
                    dve.wait_ge(unit_hi, copied(g, pos))
                    low(unit_view(kind, 1), unit_psum(kind, bk), unit_view(kind, 0)).then_inc(unit_lo, 1)

            def attention_stats(g, dst):
                final = isinstance(g, int) and g == NG - 1
                seq, number = units(g)
                pos = seq.index("W")
                bk = unit_bank[parity(g, pos)]
                dve.wait_ge(unit_done, number + pos + 1)
                ln2.start(g)
                for b in range(GB):
                    last = V.bn_stats(bn[:, 2 + b, :], bk[:, b * D:(b + 1) * D])
                ln2.count(last)
                if not final:
                    maxima(g + 1, 1)
                ln2.wait()
                settle()
                for b in range(GB):
                    last = V.bn_aggr(mv[:, 2 + b, :], bn[:, 2 + b, :])
                ln2.link(last)
                if not final:
                    wait(dve, x2_out, g * 16)
                for b in range(GB):
                    last = V.scalar_tensor_tensor(out=dst[:, b, :], in0=bk[:, b * D:(b + 1) * D],
                                                  scalar=mv[:, 2 + b, 0:1], in1=gs[:, :],
                                                  op0=ALU.subtract, op1=ALU.mult)
                last.then_inc(w_free, 1)

            def attention_rstd(g):
                ln2.start(g, 2)
                rsqrt_start(ln2.link, mv[:, 2:4, 1], [rs[:, 4 + i, :] for i in range(3)], EPS_OUT)

            def attention_norm(g, dst):
                rsqrt_end(ln2.link, [rs[:, 4 + i, :] for i in range(3)])
                ln2.end()
                dve.wait_ge(w_free, g + 2)
                dve.wait_ge(xgb_ready, g + 1)
                for b in range(GB):
                    last = V.scalar_tensor_tensor(out=dst[:, b, :], in0=dst[:, b, :], scalar=rs[:, 4, b:b + 1],
                                                  in1=xr[:, b, :], op0=ALU.mult, op1=ALU.add)
                last.then_inc(x2_ready, 1)

            def x2_statistics(g, src):
                dve.wait_ge(x2_ready, g + 1)
                settle()
                ln3.start(g)
                for b in range(GB):
                    last = V.bn_stats(bn[:, 2 + b, :], src[:, b, :])
                ln3.link(last)
                settle()
                for b in range(GB):
                    last = V.bn_aggr(mv[:, 2 + b, :], bn[:, 2 + b, :])
                ln3.link(last)
                settle()
                V.tensor_copy(mean_var[:, bass.ds(g * GB, GB), :], mv[:, 2:4, :]).then_inc(x2_stats, 1)

            def x2_range(g, src):
                V.tensor_reduce(x2_max[:, bass.ds(g * GB, GB)], src, AX.X, ALU.max)
                V.tensor_reduce(x2_min[:, bass.ds(g * GB, GB)], src, AX.X, ALU.min).then_inc(x2_stats, 1)

            def maxima(g, c):
                dve.wait_ge(scores_done, g * NS + c + 1)
                for h in range(2):
                    last = V.tensor_reduce(nmax[:, c % 2, 2 * h:2 * h + 2],
                                           score_bank[c % 2][h][:, 0:GB * QW].rearrange(
                                               "p (b s) -> p b s", b=GB)[:, :, 0:NK],
                                           AX.X, ALU.max, negate=True)
                last.then_inc(max_done, 1)

            def inverse_sums(g, c):
                wait(dve, exp_done, g * NS + c + 1)
                V.reciprocal(rinv[:, c % 2, :], rowsum[:, c % 2, :]).then_inc(rinv_done, 1)

            def prob_copy(g, c):
                dve.wait_ge(pt_done, g * (NS + 1) + c + 1)
                V.tensor_copy(pT[:, c % 2, :, :],
                              pt_bank[:, :].rearrange("p (u s) -> p u s", u=4)).then_inc(pt_copied, 1)

            def null_low(g):
                dve.wait_ge(null_hi, g + 1)
                low(nullT[1][:, :], pt_bank[0:HEADS, 0:TG], nullT[0][:, :]).then_inc(pt_copied, 1)

            def out_low(g, c):
                dve.wait_ge(ot_hi, g * NS + c + 1)
                low(oT[1][:, c, :], pv_bank[:, 0:TG], oT[0][:, c, :]).then_inc(ot_lo, 1)

            def weight_scales(m):
                dve.wait_ge(fraw_in[m], 16)
                wait(dve, fw_ready, m)
                w = fraw[:, m, :, :]
                V.tensor_reduce(fs[:, 0, :], w, AX.X, ALU.max, apply_absolute_value=True).then_inc(fchain, 1)
                dve.wait_ge(fchain, 3 * m + 1)
                V.tensor_scalar(fs[:, 0, :], fs[:, 0, :], 1.0 / WMAX, MIN_SCALE, ALU.mult, ALU.max).then_inc(fchain, 1)
                dve.wait_ge(fchain, 3 * m + 2)
                V.reciprocal(fs[:, 1, :], fs[:, 0, :]).then_inc(fchain, 1)
                dve.wait_ge(fchain, 3 * m + 3)

            def weight_integers(m):
                bc = fs[:, 1, :].rearrange("p (n o) -> p n o", o=1).to_broadcast([P, NBK, WBLOCK])
                V.tensor_tensor(fint[:, :, :], fraw[:, m, :, :], bc, ALU.mult).then_inc(fint_ready, 1)

            def weight_values(m):
                bc = fs[:, 0, :].rearrange("p (n o) -> p n o", o=1).to_broadcast([P, NBK, WBLOCK])
                dve.wait_ge(fint_ready, m + 1)
                V.tensor_tensor(fraw[:, m, :, :], fint[:, :, :], bc, ALU.mult).then_inc(fw_ready, 1)

            V.memset(ones[:, :], 1.0)
            V.memset(nkw[:, :, :], 0.0).then_inc(prep_chain, 1)
            V.memset(nvm[:, :, :], 0.0).then_inc(prep_chain, 1)
            ln_stats(0)
            ln_rstd()
            ln_apply()
            npos = [0]

            def constants():
                dve.wait_ge(tanh_done, 1)
                dve.wait_ge(prep_chain, 2)
                V.tensor_scalar(gs[:, :], gs[:, :], gates[:, 0:1], None, ALU.mult)
                V.tensor_scalar(gb[:, :], gb[:, :], gates[:, 0:1], None, ALU.mult).then_inc(const_ready, 1)
                V.tensor_scalar(nkw[:, :, 0:1], nkw[:, :, 0:1], ncol[:, 0:1], None, ALU.add)
                diag = nvm[:, :, :].rearrange("p k h -> p (k h)")
                for h in range(2):
                    rows = slice(h * DH, (h + 1) * DH)
                    d = diag[rows, h:h + (HEADS + 2) * (KF - 1) + 1:HEADS + 2]
                    last = V.tensor_scalar(d, d, ncol[rows, 1:2], None, ALU.add)
                last.then_inc(prep_chain, 1)
                dve.wait_ge(prep_chain, 3)
                V.tensor_copy(qk[:, :, GB:2 * GB, S:QW],
                              nkw[:, :, :].rearrange("p (c b) t -> p c b t", b=GB)).then_inc(null_ready, 1)
                V.tensor_copy(nvr[0][:, :, :], nvm[:, :, :]).then_inc(prep_chain, 1)
                dve.wait_ge(prep_chain, 4)
                low(nvr[1][:, :, :], nvm[:, :, :], nvr[0][:, :, :]).then_inc(null_ready, 1)

            for i, (dst, _, f, fold) in enumerate(pieces):
                for _ in range(PRO_BEFORE.get(i, 0)):
                    split("pro", npos[0])
                    npos[0] += 1
                if i == READY_K:
                    constants()
                dve.wait_ge(wsplit_hi, i + 1)
                low(dst[1], stage_view(i, fold), dst[0], f).then_inc(wsplit_lo, 1)
            while npos[0] < len(PRO):
                if PRO[npos[0]] == "V00":
                    ln_stats(1)
                    ln_rstd()
                    ln_apply()
                    weight_scales(0)
                elif PRO[npos[0]] == "W":
                    weight_integers(0)
                split("pro", npos[0])
                if PRO[npos[0]] == "k6":
                    maxima(0, 0)
                    inverse_sums(0, 0)
                npos[0] += 1

            maxima(0, 1)
            dve.wait_ge(const_ready, 1)

            def group(g):
                peeled, final = isinstance(g, int), isinstance(g, int) and g == NG - 1
                first = peeled and g == 0
                pos, (steps, tail) = 0, plan(g)
                for c in range(NS):
                    if 1 <= c < NS - 1:
                        maxima(g, c + 1)
                    if c == 1 and not first:
                        attention_rstd(g - 1)
                    if c == 2 and not first:
                        attention_norm(g - 1, y)
                    if c == 3 and not first:
                        x2_statistics(g - 1, y[:, :, :])
                    if c == 4 and feeds(g):
                        ln_stats(g + 2)
                    if c == 5 and feeds(g):
                        ln_rstd()
                    if c == 6 and feeds(g):
                        ln_apply()
                    if first and c == 0:
                        weight_values(0)
                    if first and 1 <= c < 4:
                        (weight_scales, weight_integers, weight_values)[c - 1](1)
                    if peeled and g == NG - 2 and 4 <= c < 7:
                        (weight_scales, weight_integers, weight_values)[c - 4](2)
                    weights = steps[c][0][0:1] == "F"
                    if c < NS - 1 and not weights:
                        inverse_sums(g, c + 1)
                    if c == NS - 1:
                        prob_copy(g, c)
                        out_low(g, c - 1)
                    for _ in steps[c]:
                        split(g, pos)
                        pos += 1
                    if c < NS - 1 and weights:
                        inverse_sums(g, c + 1)
                    if c < NS - 1:
                        prob_copy(g, c)
                    if 0 < c < NS - 1:
                        out_low(g, c - 1)
                if not final:
                    maxima(g + 1, 0)
                    inverse_sums(g + 1, 0)
                out_low(g, NS - 1)
                for u in tail:
                    if u == "null":
                        null_low(g)
                        continue
                    split(g, pos)
                    pos += 1
                    if u in ("Ca", "V10", "F8") and not first:
                        x2_range(g - 1, y[:, :, :])
                attention_stats(g, last2 if final else y)

            last2 = x2all[:, (NG - 1) * GB:, :]
            group(0)
            with dve.Fori(1, LOOPED) as g:
                group(g)
            group(NG - 2)
            group(NG - 1)
            attention_rstd(NG - 1)
            attention_norm(NG - 1, last2)

            g = NG - 1
            dve.wait_ge(x2_ready, NG)
            x2_statistics(g, last2)
            x2_range(g, last2)

            fc = [9]

            def link(ins):
                fc[0] += 1
                ins.then_inc(fchain, 1)
                dve.wait_ge(fchain, fc[0])

            def s1(i):
                return small[:, i:i + 1]

            def global_max(n):
                dve.wait_ge(gm_1, n + 1)
                V.reduce_max(small[0:1, 1:2], bank[0][0:1, 0:P], AX.X).then_inc(gm_t, 1)
                dve.wait_ge(gm_b, n + 1)

            dve.wait_ge(x2_stats, 2 * NG)
            r = [rs3[:, i, :] for i in range(3)]
            rsqrt_start(link, mean_var[:, :, 1], r, EPS_LN)
            rsqrt_end(link, r)
            link(V.tensor_tensor(fa[:, 0, :], x2_max[:, :], mean_var[:, :, 0], ALU.subtract))
            link(V.tensor_tensor(fa[:, 1, :], mean_var[:, :, 0], x2_min[:, :], ALU.subtract))
            link(V.tensor_tensor(fa[:, 0, :], fa[:, 0, :], fa[:, 1, :], ALU.max))
            link(V.tensor_tensor(fa[:, 0, :], fa[:, 0, :], rs3[:, 0, :], ALU.mult))
            V.reduce_max(s1(0), fa[:, 0, :], AX.X).then_inc(gm_t, 1)
            global_max(0)
            link(V.tensor_scalar(s1(4), bank[1][:, 0:1], 1.0 / QMAX, MIN_SCALE, ALU.mult, ALU.max))
            link(V.reciprocal(s1(5), s1(4)))
            link(V.tensor_scalar(fa[:, 2, :], rs3[:, 0, :], s1(5), None, ALU.mult))
            link(V.scalar_tensor_tensor(out=fa[:, 3, :], in0=mean_var[:, :, 0], scalar=-1.0, in1=fa[:, 2, :],
                                        op0=ALU.mult, op1=ALU.mult))
            V.memset(pause[:, :], 0.0).then_inc(xaffine, 1)
            dve.wait_ge(x2all_in, 16)
            for b in range(2):
                last = V.tensor_scalar(xi[:, 0, b, :], x2all[:, b, :], fa[:, 2, b:b + 1], fa[:, 3, b:b + 1],
                                       ALU.mult, ALU.add)
            last.then_inc(xi_first, 1)

            def x_low(t):
                dve.wait_ge(xt_hi, t + 1)
                low(xT[1][:, :, t * TG:(t + 1) * TG], unit_bank[t % 2][:, :].rearrange("p (k s) -> p k s", k=KD),
                    xT[0][:, :, t * TG:(t + 1) * TG]).then_inc(xt_lo, 1)

            def gu_maximum(m, n):
                tg, j = n // KI, n % KI
                q = m * 4 * KI + n
                dve.wait_ge(gu_out, q + 1)
                src = (gate, up)[m][:, j, tg * 512:(tg + 1) * 512]
                if m == 0:
                    V.tensor_reduce(amax[:, 0, n:n + 1], src, AX.X, ALU.max)
                    return V.tensor_reduce(amax[:, 0, 4 * KI + n:4 * KI + n + 1], src, AX.X, ALU.min, negate=True)
                return V.tensor_reduce(amax[:, 1, n:n + 1], src, AX.X, ALU.max, apply_absolute_value=True)

            def scale_column(src):
                V.reduce_max(s1(0), src, AX.X).then_inc(gm_t, 1)

            def scale_row(n):
                dve.wait_ge(gm_1, n + 1)
                V.reduce_max(small[0:1, 1:2], bank[0][0:1, 0:P], AX.X).then_inc(gm_t, 1)

            def scale_values(n, factor_q, s, r, factor):
                dve.wait_ge(gm_b, n + 1)
                link(V.tensor_scalar(s1(s), bank[1][:, 0:1], factor_q, MIN_SCALE, ALU.mult, ALU.max))
                link(V.reciprocal(s1(3), s1(s)))
                V.tensor_scalar(s1(r), s1(3), factor, None, ALU.mult).then_inc(scale_ready, 1)

            def scale(n, src, factor_q, s, r, factor):
                scale_column(src)
                scale_row(n)
                scale_values(n, factor_q, s, r, factor)

            link(V.tensor_scalar(s1(7), s1(4), 1.0 / QMAX, None, ALU.mult))
            for t in range(2):
                x_low(t)
            for n in range(4 * KI):
                last = gu_maximum(0, n)
                if n in (1, 3):
                    x_low(2 + n // 2)
                if n in (KI - 1, 2 * KI - 1):
                    x_low(4 + 2 * (n // KI))
                    x_low(5 + 2 * (n // KI))
            link(last)
            link(V.reduce_max(s1(6), amax[:, 0, 0:4 * KI], AX.X))
            scale(1, amax[:, 0, :], s1(7), 10, 11, s1(4))
            link(V.tensor_scalar(s1(14), s1(10), 1.0 / 65536.0, None, ALU.mult))
            link(V.tensor_scalar(s1(8), s1(14), 1.0 / QMAX, None, ALU.mult))
            gate_c = gate[:, :, :].rearrange("p j t -> p (j t)")
            up_c = up[:, :, :].rearrange("p j t -> p (j t)")

            ahead = 5
            for q in range(ahead):
                gu_maximum(1, q).then_inc(gu_max, 1)
            for q in range(4 * KI):
                if by_vector(q):
                    dve.wait_ge(sg_ready, q + 1)
                    link(V.tensor_scalar(tsi[:, q % GS, :], tsg[:, q % 4, :], 65536.0, None, ALU.mult))
                else:
                    dve.wait_ge(si_ready, pool_made(q))
                V.tensor_tensor_reduce(gate_piece(q), tgi[:, q % GS, :], tsi[:, q % GS, :], -1.0, 0.0,
                                       ALU.mult, ALU.max, amax[:, 2, q:q + 1]).then_inc(p_ready, 1)
                if q + ahead < 4 * KI:
                    gu_maximum(1, q + ahead).then_inc(gu_max, 1)
                if q == 4 * KI - 4:
                    dve.wait_ge(gu_max, 4 * KI)
                    scale_column(amax[:, 1, 0:4 * KI])
                if q == 4 * KI - 3:
                    scale_row(2)
                if q == 4 * KI - 2:
                    scale_values(2, s1(7), 13, 12, s1(4))
            dve.wait_ge(si_ready, pool_made(4 * KI))
            V.tensor_tensor(amax[:, 2, 4 * KI:4 * KI + 1], tgi[:, 4 * KI % GS, 0:1], tsi[:, 4 * KI % GS, 0:1],
                            ALU.mult).then_inc(p_ready, 1)
            dve.wait_ge(p_ready, 4 * KI + 1)
            scale(3, amax[:, 2, 0:4 * KI + 1], s1(8), 15, 16, s1(14))
            link(V.tensor_scalar(s1(17), s1(15), s1(13), None, ALU.mult))
            link(V.tensor_scalar(s1(9), s1(17), 1.0 / QMAX, None, ALU.mult))
            for q in range(NCH):
                dve.wait_ge(ui_ready, q + 1)
                wait(dve, o_ready, q - 1)
                if magnitude_by_scalar(q):
                    dve.wait_ge(pi_scalar, sum(magnitude_by_scalar(i) for i in range(q + 1)))
                    V.tensor_tensor_reduce(prod[:, q % 2, :], tpi[:, q % 4, :], tui[:, q % 4, :], 1.0, 0.0,
                                           ALU.mult, ALU.max, amax[:, 3, q:q + 1]).then_inc(o_ready, 1)
                else:
                    dve.wait_ge(pi_pool, q // 3 + 1)
                    link(V.tensor_tensor(prod[:, q % 2, :], tpi[:, q % 4, :], tui[:, q % 4, :], ALU.mult))
                    V.tensor_reduce(amax[:, 3, q:q + 1], prod[:, q % 2, :], AX.X, ALU.max,
                                    apply_absolute_value=True).then_inc(o_ready, 1)
            dve.wait_ge(o_ready, NCH)
            scale(4, amax[:, 3, 0:NCH], s1(9), 18, 19, s1(17))
            V.tensor_scalar(s1(20), s1(18), gates[:, 1:2], None, ALU.mult).then_inc(scale_ready, 1)
            dve.wait_ge(scale_ready, 5)

            def o_integers(n):
                dve.wait_ge(ti_ready, n + 1)
                dve.wait_ge(tu_ready, n + 1)
                wait(dve, ol_ready, n - 3)
                V.scalar_tensor_tensor(out=oint(n), in0=tgi[:, n % GS, :], scalar=s1(19), in1=ui(n), op0=ALU.mult,
                                       op1=ALU.mult).then_inc(oi_ready, 1)

            for n in range(2):
                o_integers(n)
            for n in range(4 * KI):
                tg, j = n // KI, n % KI
                if n + 2 < 4 * KI:
                    o_integers(n + 2)
                dve.wait_ge(oh_ready, n + 1)
                low(oI[1][:, tg % 2, j, :], oint(n), oI[0][:, tg % 2, j, :]).then_inc(ol_ready, 1)
            for t in range(6, 8):
                dve.wait_ge(down_done, 2 * t + 2)
                dve.wait_ge(xlast_in, 16)
                for b in range(2):
                    last = V.scalar_tensor_tensor(out=xlast[:, t % 2, b, :], in0=bank[(2 * t + b) % 8][:, 0:D],
                                                  scalar=s1(20), in1=xlast[:, t % 2, b, :], op0=ALU.mult, op1=ALU.add)
                last.then_inc(y_last, 1)

        @block.gpsimd
        def _(pool):
            G = nc.gpsimd
            row = lambda a: a.rearrange("(o n) -> o n", o=1)
            G.memset(ident[:, :], 0.0).then_inc(ident_zero, 1)
            pool.wait_ge(ident_zero, 1)
            G.affine_select(out=ident[:, :], in_=ident[:, :], compare_op=ALU.not_equal, fill=1.0, base=0,
                            pattern=[[-1, P]], channel_multiplier=1).then_inc(ident_ready, 1)
            pool.dma_start(gates[:, 0:1], row(g_xattn).to_broadcast([P, 1])).then_inc(const_in, 16)
            pool.dma_start(gates[:, 1:2], row(g_ffn).to_broadcast([P, 1])).then_inc(const_in, 16)
            pool.dma_start(gs[:, :], row(ln_scale).to_broadcast([P, D])).then_inc(const_in, 16)
            pool.dma_start(gb[:, :], row(ln_bias).to_broadcast([P, D])).then_inc(const_in, 16)
            with nc.allow_non_contiguous_dma(reason="one null key and value, 128 numbers"):
                for h in range(2):
                    pool.dma_start(ncol[h * DH:(h + 1) * DH, :], null_kv.rearrange("t d -> d t")).then_inc(const_in, 16)

            def normalise(g, c):
                pool.wait_ge(rinv_done, g * NS + c + 1)
                G.tensor_tensor(probs[:, c % 2, :, 0:S], probs[:, c % 2, :, 0:S],
                                rinv[:, c % 2, :].rearrange("p (u o) -> p u o", o=1).to_broadcast([P, 4, S]),
                                ALU.mult).then_inc(norm_done, 1)
                if c == 0 and not (isinstance(g, int) and g == 0):
                    wait(pool, pt_done, g * (NS + 1))
                G.tensor_tensor(pnull[:, :, 2 * c:2 * c + 2].rearrange("p b h -> p h b"),
                                probs[:, c % 2, :, S].rearrange("p (h b) -> p h b", h=2),
                                rinv[:, c % 2, :].rearrange("p (h b) -> p h b", h=2), ALU.mult).then_inc(pnull_done, 1)

            normalise(0, 0)
            pool.wait_ge(const_ready, 1)

            def group(g):
                for c in range(1, NS):
                    if c == 6:
                        pool.wait_ge(xres_in, 16 * (g + 1))
                        G.tensor_tensor(xr[:, :, :], xr[:, :, :],
                                        gb[:, :].rearrange("p (o d) -> p o d", o=1).to_broadcast([P, GB, D]),
                                        ALU.add).then_inc(xgb_ready, 1)
                    normalise(g, c)
                if not (isinstance(g, int) and g == NG - 1):
                    normalise(g + 1, 0)

            group(0)
            with pool.Fori(1, LOOPED) as g:
                group(g)
            group(NG - 2)
            group(NG - 1)

            pool.wait_ge(xaffine, 1)
            pool.wait_ge(x2all_in, 16)
            for t in range(1, NT // 2):
                if t >= 2:
                    pool.wait_ge(xf_ready, t - 1)
                for b in range(2):
                    n = 2 * t + b
                    last = G.tensor_scalar(xi[:, t % 2, b, :], x2all[:, n, :], fa[:, 2, n:n + 1], fa[:, 3, n:n + 1],
                                           ALU.mult, ALU.add)
                last.then_inc(xi_ready, 1)

            gate_c = gate[:, :, :].rearrange("p j t -> p (j t)")
            up_c = up[:, :, :].rearrange("p j t -> p (j t)")
            pool.wait_ge(scale_ready, 1)

            def gate_integers(q):
                if q >= GS:
                    pool.wait_ge(p_ready, q - GS + 1)
                n, src = (HC, gate_piece(q)) if q < 4 * KI else (1, small[:, 6:7])
                G.tensor_scalar(tgi[:, q % GS, 0:n], src, small[:, 11:12], 1.0, ALU.mult,
                                ALU.mult).then_inc(gi_ready, 1)

            def sigmoid_integers(q):
                n = HC if q < 4 * KI else 1
                pool.wait_ge(sg_ready, q + 1)
                G.tensor_scalar(tsi[:, q % GS, 0:n], tsg[:, q % 4, 0:n], 65536.0, 1.0, ALU.mult,
                                ALU.mult).then_inc(si_ready, 1)

            for q in range(4):
                gate_integers(q)
            for q in range(4 * KI + 1):
                if not by_vector(q):
                    sigmoid_integers(q)
                if q + 4 <= 4 * KI:
                    gate_integers(q + 4)

            pool.wait_ge(scale_ready, 3)
            for q in range(0, NCH, 3):
                if q >= 4:
                    pool.wait_ge(o_ready, q - 3)
                G.tensor_scalar(tpi[:, q % 4, :], gate_c[:, q * CH:(q + 1) * CH], small[:, 16:17], -1.0,
                                ALU.mult, ALU.mult).then_inc(pi_pool, 1)

            def finish(t):
                pool.wait_ge(fin_scaled, t + 1)
                pool.wait_ge(xres_ld[t % 2], 16 * (t // 2 + 1))
                G.tensor_tensor(yout[:, t % 2, :, :], yout[:, t % 2, :, :], xres[:, t % 2, :, :],
                                ALU.add).then_inc(y_ready, 1)

            for n in range(4 * KI):
                tg, j = n // KI, n % KI
                if n >= GS:
                    pool.wait_ge(oi_ready, n - GS + 1)
                G.tensor_scalar(tgi[:, n % GS, :], gate_piece(n), small[:, 16:17], -1.0, ALU.mult,
                                ALU.mult).then_inc(ti_ready, 1)
                if tg >= 2 and j in (3, 5):
                    finish(2 * tg - 5 + j // 2)
            for t in range(4, 6):
                finish(t)


_INS = ['x', 'ctx_2048', 'g_xattn', 'g_ffn', 'L0_xattn_Wq', 'L0_xattn_Wkv', 'L0_xattn_null_kv', 'L0_xattn_Wout',
        'L0_xattn_ln_scale', 'L0_xattn_ln_bias', 'L0_ffn_w_gate', 'L0_ffn_w_up', 'L0_ffn_w_down']


def kernel(**inputs):
    import numpy as _np
    import concourse.bacc as _bacc
    from concourse import mybir as _mybir
    from concourse.bass_utils import run_bass_kernel_spmd as _run

    nc = _bacc.Bacc("TRN2", target_bir_lowering=False, num_devices=1)
    arrays, args = {}, []
    for name in _INS:
        a = _np.ascontiguousarray(inputs[name])
        arrays[f"in_{name}"] = a
        args.append(nc.dram_tensor(f"in_{name}", a.shape, _mybir.dt.from_np(a.dtype), kind="ExternalInput").ap())
    shape = arrays["in_x"].shape
    args.append(nc.dram_tensor("out_0", shape, _mybir.dt.float32, kind="ExternalOutput").ap())
    gated_cross_attention_ffn(nc, *args)
    return _run(nc, [arrays], core_ids=[0]).results[0]["out_0"]
```
